# Optimizing a Trainium2 kernel written in Bass

```python
import numpy as np
import jax
import jax.numpy as jnp

def _softmax(x, axis=-1):
    return jax.nn.softmax(x, axis=axis)

def _gelu(x):
    return jax.nn.gelu(x, approximate=True)

def _silu(x):
    return jax.nn.silu(x)

def _sigmoid(x):
    return jax.nn.sigmoid(x)

def _layernorm(x, axis=-1, eps=1e-05):
    m = jnp.mean(x, axis=axis, keepdims=True)
    v = jnp.var(x, axis=axis, keepdims=True)
    return (x - m) / jnp.sqrt(v + eps)

def _scatter_add(tgt, idx, src, axis=0):
    return tgt.at[idx].add(src)

def _segment_sum(src, seg, n):
    return jax.ops.segment_sum(src, seg, n)
kernel_name = 'mk_adj_resnorm_d4_adj_r2_ac0af1'

def setup_inputs(seed: int=0):
    np.random.seed(seed)
    _w = jnp.asarray

    def _rec_inputs():
        import jax
        import jax.numpy as jnp
        _gk = jax.random.key(seed)
        x = -0.0003929 + 0.9999 * jax.random.normal(jax.random.fold_in(_gk, 1), (16, 512, 256), jnp.float32)
        _a = jax.random.bernoulli(jax.random.fold_in(_gk, 2), 0.03125, (512, 512))
        _a = jnp.logical_or(_a, jnp.swapaxes(_a, -1, -2))
        _a = jnp.logical_or(_a, jnp.eye(512, dtype=bool))
        _af = _a.astype(jnp.float32)
        _af = _af * jax.random.uniform(jax.random.fold_in(_gk, 3), (512, 512), jnp.float32, 0.05, 1)
        adj = _af
        return (x, adj)
    x, adj = _rec_inputs()

    def _L0_gnn_setup():
        import jax, jax.numpy as jnp
        import numpy as np
        B, N, F_IN, F_OUT = (16, 1024, 256, 256)
        key = jax.random.key(seed)
        k1, k2, k3 = jax.random.split(key, 3)
        x = jax.random.normal(k1, (B, N, F_IN), dtype=jnp.float32)
        adj = jax.random.uniform(k2, (N, N), dtype=jnp.float32)
        bound = np.sqrt(6.0 / F_OUT)
        weight = jax.random.uniform(k3, (F_IN, F_OUT), dtype=jnp.float32, minval=-bound, maxval=bound)
        bias = jnp.zeros((F_OUT,), dtype=jnp.float32)
        return {'x': x, 'adj': adj, 'weight': weight, 'bias': bias}
    _L0_gnn_all = _L0_gnn_setup()
    _L0_gnn_in = {k: v for k, v in _L0_gnn_all.items() if k in ('weight', 'bias')}
    del _L0_gnn_all

    def _L1_gnn_setup():
        import jax, jax.numpy as jnp
        import numpy as np
        B, N, D, H = (16, 1025, 256, 8)
        LN_EPS = 1e-05

        def _make_mask(key, n):
            n_proto = n - 1
            adj = jax.random.bernoulli(key, 0.03, (n_proto, n_proto)).astype(jnp.float32)
            adj = jnp.clip(adj + adj.T + jnp.eye(n_proto, dtype=jnp.float32), 0.0, 1.0)
            mask = jnp.zeros((n, n), dtype=jnp.float32)
            mask = mask.at[0, :].set(1.0).at[:, 0].set(1.0)
            mask = mask.at[1:, 1:].set(adj)
            return mask
        key = jax.random.key(seed)
        ks = jax.random.split(key, 7)
        s = 1.0 / np.sqrt(D)
        return {'x': jax.random.normal(ks[0], (B, N, D), dtype=jnp.float32), 'w_qkv': jax.random.uniform(ks[1], (D, 3 * D), dtype=jnp.float32, minval=-s, maxval=s), 'w_proj': jax.random.uniform(ks[2], (D, D), dtype=jnp.float32, minval=-s, maxval=s), 'b_proj': jnp.zeros((D,), dtype=jnp.float32), 'ln_gamma': jnp.ones((D,), dtype=jnp.float32), 'ln_beta': jnp.zeros((D,), dtype=jnp.float32), 'attn_mask': _make_mask(ks[3], N)}
    _L1_gnn_all = _L1_gnn_setup()
    _L1_gnn_in = {k: v for k, v in _L1_gnn_all.items() if k in ('w_qkv', 'w_proj', 'b_proj', 'ln_gamma', 'ln_beta')}
    del _L1_gnn_all

    def _L2_gnn_setup():
        import jax, jax.numpy as jnp
        import numpy as np
        B, N, D, T = (64, 128, 256, 3)

        def _lin(v, W, b):
            return jnp.einsum('...i,oi->...o', v, W) + b
        key = jax.random.key(seed)
        ks = jax.random.split(key, 12)
        s2 = 1.0 / np.sqrt(2 * D)
        s1 = 1.0 / np.sqrt(D)
        return {'x': jax.random.normal(ks[0], (B, N, D), jnp.float32), 'in_mat': jax.random.uniform(ks[1], (N, N), jnp.float32) / N, 'out_mat': jax.random.uniform(ks[2], (N, N), jnp.float32) / N, 'w3_w': jax.random.normal(ks[3], (D, 2 * D), jnp.float32) * s2, 'w3_b': jnp.zeros((D,), jnp.float32), 'u3_w': jax.random.normal(ks[4], (D, D), jnp.float32) * s1, 'u3_b': jnp.zeros((D,), jnp.float32), 'w4_w': jax.random.normal(ks[5], (D, 2 * D), jnp.float32) * s2, 'w4_b': jnp.zeros((D,), jnp.float32), 'w5_w': jax.random.normal(ks[6], (D, 2 * D), jnp.float32) * s2, 'w5_b': jnp.zeros((D,), jnp.float32), 'u5_w': jax.random.normal(ks[7], (D, D), jnp.float32) * s1, 'u5_b': jnp.zeros((D,), jnp.float32)}
    _L2_gnn_all = _L2_gnn_setup()
    _L2_gnn_in = {k: v for k, v in _L2_gnn_all.items() if k in ('w3_w', 'w3_b', 'u3_w', 'u3_b', 'w4_w', 'w4_b', 'w5_w', 'w5_b', 'u5_w', 'u5_b')}
    del _L2_gnn_all

    def _L3_gnn_setup():
        import jax, jax.numpy as jnp
        import numpy as np
        B, N, D, H = (4, 1024, 256, 8)
        HD = D // H
        key = jax.random.key(seed)
        ks = jax.random.split(key, 10)
        x = jax.random.normal(ks[0], (B, N, D), dtype=jnp.float32)
        adj = (jax.random.uniform(ks[1], (N, N)) < 0.1).astype(jnp.float32)
        s = 1.0 / np.sqrt(D)
        Wq = jax.random.normal(ks[2], (D, D), dtype=jnp.float32) * s
        Wk = jax.random.normal(ks[3], (D, D), dtype=jnp.float32) * s
        Wv = jax.random.normal(ks[4], (D, D), dtype=jnp.float32) * s
        Wo = jax.random.normal(ks[5], (D, D), dtype=jnp.float32) * s
        bq = jnp.zeros((D,), jnp.float32)
        bk = jnp.zeros((D,), jnp.float32)
        bv = jnp.zeros((D,), jnp.float32)
        bo = jnp.zeros((D,), jnp.float32)
        return {'x': x, 'adj': adj, 'Wq': Wq, 'bq': bq, 'Wk': Wk, 'bk': bk, 'Wv': Wv, 'bv': bv, 'Wo': Wo, 'bo': bo}
    _L3_gnn_all = _L3_gnn_setup()
    _L3_gnn_in = {k: v for k, v in _L3_gnn_all.items() if k in ('Wq', 'bq', 'Wk', 'bk', 'Wv', 'bv', 'Wo', 'bo')}
    del _L3_gnn_all
    return {'x': x, 'adj': adj, 'L0_gnn_weight': _L0_gnn_in['weight'], 'L0_gnn_bias': _L0_gnn_in['bias'], 'L1_gnn_w_qkv': _L1_gnn_in['w_qkv'], 'L1_gnn_w_proj': _L1_gnn_in['w_proj'], 'L1_gnn_b_proj': _L1_gnn_in['b_proj'], 'L1_gnn_ln_gamma': _L1_gnn_in['ln_gamma'], 'L1_gnn_ln_beta': _L1_gnn_in['ln_beta'], 'L2_gnn_w3_w': _L2_gnn_in['w3_w'], 'L2_gnn_w3_b': _L2_gnn_in['w3_b'], 'L2_gnn_u3_w': _L2_gnn_in['u3_w'], 'L2_gnn_u3_b': _L2_gnn_in['u3_b'], 'L2_gnn_w4_w': _L2_gnn_in['w4_w'], 'L2_gnn_w4_b': _L2_gnn_in['w4_b'], 'L2_gnn_w5_w': _L2_gnn_in['w5_w'], 'L2_gnn_w5_b': _L2_gnn_in['w5_b'], 'L2_gnn_u5_w': _L2_gnn_in['u5_w'], 'L2_gnn_u5_b': _L2_gnn_in['u5_b'], 'L3_gnn_Wq': _L3_gnn_in['Wq'], 'L3_gnn_bq': _L3_gnn_in['bq'], 'L3_gnn_Wk': _L3_gnn_in['Wk'], 'L3_gnn_bk': _L3_gnn_in['bk'], 'L3_gnn_Wv': _L3_gnn_in['Wv'], 'L3_gnn_bv': _L3_gnn_in['bv'], 'L3_gnn_Wo': _L3_gnn_in['Wo'], 'L3_gnn_bo': _L3_gnn_in['bo']}

def reference(x, adj, L0_gnn_weight, L0_gnn_bias, L1_gnn_w_qkv, L1_gnn_w_proj, L1_gnn_b_proj, L1_gnn_ln_gamma, L1_gnn_ln_beta, L2_gnn_w3_w, L2_gnn_w3_b, L2_gnn_u3_w, L2_gnn_u3_b, L2_gnn_w4_w, L2_gnn_w4_b, L2_gnn_w5_w, L2_gnn_w5_b, L2_gnn_u5_w, L2_gnn_u5_b, L3_gnn_Wq, L3_gnn_bq, L3_gnn_Wk, L3_gnn_bk, L3_gnn_Wv, L3_gnn_bv, L3_gnn_Wo, L3_gnn_bo):
    import jax
    import jax.numpy as jnp

    def _L0_gnn_ref(x, adj, weight, bias):
        import jax, jax.numpy as jnp
        import numpy as np
        B, N, F_IN, F_OUT = (16, 1024, 256, 256)
        deg = adj.sum(axis=1)
        deg_inv_sqrt = jnp.where(deg > 0, jax.lax.rsqrt(deg), 0.0)
        norm_adj = adj * deg_inv_sqrt[:, None] * deg_inv_sqrt[None, :]
        support = jnp.einsum('bni,io->bno', x, weight)
        output = jnp.einsum('nm,bmo->bno', norm_adj, support)
        return output + bias

    def _L1_gnn_ref(x, w_qkv, w_proj, b_proj, ln_gamma, ln_beta, attn_mask):
        import jax, jax.numpy as jnp
        import numpy as np
        B, N, D, H = (16, 1025, 256, 8)
        LN_EPS = 1e-05

        def _make_mask(key, n):
            n_proto = n - 1
            adj = jax.random.bernoulli(key, 0.03, (n_proto, n_proto)).astype(jnp.float32)
            adj = jnp.clip(adj + adj.T + jnp.eye(n_proto, dtype=jnp.float32), 0.0, 1.0)
            mask = jnp.zeros((n, n), dtype=jnp.float32)
            mask = mask.at[0, :].set(1.0).at[:, 0].set(1.0)
            mask = mask.at[1:, 1:].set(adj)
            return mask
        b, n, d = x.shape
        hd = d // H
        scale = hd ** (-0.5)
        qkv = (x @ w_qkv).reshape(b, n, 3, H, hd).transpose(2, 0, 3, 1, 4)
        q, k, v = (qkv[0], qkv[1], qkv[2])
        attn = jnp.einsum('bhnd,bhmd->bhnm', q, k) * scale
        attn = jnp.where(attn_mask[None, None] == 0, -jnp.inf, attn)
        attn = jax.nn.softmax(attn, axis=-1)
        o = jnp.einsum('bhnm,bhmd->bhnd', attn, v).transpose(0, 2, 1, 3).reshape(b, n, d)
        o = o @ w_proj + b_proj
        mu = jnp.mean(o, axis=-1, keepdims=True)
        var = jnp.mean(jnp.square(o - mu), axis=-1, keepdims=True)
        ln = (o - mu) * jax.lax.rsqrt(var + LN_EPS) * ln_gamma + ln_beta
        return o + ln

    def _L2_gnn_ref(x, in_mat, out_mat, w3_w, w3_b, u3_w, u3_b, w4_w, w4_b, w5_w, w5_b, u5_w, u5_b):
        import jax, jax.numpy as jnp
        import numpy as np
        B, N, D, T = (64, 128, 256, 3)

        def _lin(v, W, b):
            return jnp.einsum('...i,oi->...o', v, W) + b
        h = x
        for _ in range(T):
            a_in = jnp.einsum('nm,bmd->bnd', in_mat, h)
            a_out = jnp.einsum('nm,bmd->bnd', out_mat, h)
            av = jnp.concatenate([a_in, a_out], axis=-1)
            z = jax.nn.sigmoid(_lin(av, w3_w, w3_b) + _lin(h, u3_w, u3_b))
            r = jax.nn.sigmoid(_lin(av, w4_w, w4_b) + _lin(h, u3_w, u3_b))
            hv = jnp.tanh(_lin(av, w5_w, w5_b) + _lin(r * h, u5_w, u5_b))
            h = (1.0 - z) * h + z * hv
        return h

    def _L3_gnn_ref(x, adj, Wq, bq, Wk, bk, Wv, bv, Wo, bo):
        import jax, jax.numpy as jnp
        import numpy as np
        B, N, D, H = (4, 1024, 256, 8)
        HD = D // H
        b, n, d = x.shape
        q = (x @ Wq + bq).reshape(b, n, H, HD)
        k = (x @ Wk + bk).reshape(b, n, H, HD)
        v = (x @ Wv + bv).reshape(b, n, H, HD)
        scores = jnp.einsum('bqhd,bkhd->bhqk', q, k) / jnp.sqrt(jnp.float32(HD))
        scores = scores + (1.0 - adj)[None, None, :, :] * -1000000000.0
        attn = jax.nn.softmax(scores, axis=-1)
        out = jnp.einsum('bhqk,bkhd->bqhd', attn, v).reshape(b, n, d)
        return out @ Wo + bo
    x = _layernorm(x + _L0_gnn_ref(x, adj, L0_gnn_weight, L0_gnn_bias), axis=-1)
    x = _layernorm(x + _L1_gnn_ref(x, L1_gnn_w_qkv, L1_gnn_w_proj, L1_gnn_b_proj, L1_gnn_ln_gamma, L1_gnn_ln_beta, adj), axis=-1)
    x = _layernorm(x + _L2_gnn_ref(x, adj, adj, L2_gnn_w3_w, L2_gnn_w3_b, L2_gnn_u3_w, L2_gnn_u3_b, L2_gnn_w4_w, L2_gnn_w4_b, L2_gnn_w5_w, L2_gnn_w5_b, L2_gnn_u5_w, L2_gnn_u5_b), axis=-1)
    x = _layernorm(x + _L3_gnn_ref(x, adj, L3_gnn_Wq, L3_gnn_bq, L3_gnn_Wk, L3_gnn_bk, L3_gnn_Wv, L3_gnn_bv, L3_gnn_Wo, L3_gnn_bo), axis=-1)
    return x

_drawn_inputs = setup_inputs


def setup_inputs(seed=0):
    import zlib

    import numpy as np

    out = dict(_drawn_inputs(seed))
    spreads = {'L0_gnn_bias': (0.0, 0.1),
     'L1_gnn_b_proj': (0.0, 0.1),
     'L1_gnn_ln_gamma': (1.0, 0.2),
     'L1_gnn_ln_beta': (0.0, 0.1),
     'L2_gnn_w3_b': (0.0, 0.38),
     'L2_gnn_u3_b': (0.0, 0.329),
     'L2_gnn_w4_b': (0.0, 2.0),
     'L2_gnn_w5_b': (0.0, 0.1),
     'L2_gnn_u5_b': (0.0, 0.1),
     'L3_gnn_bq': (0.0, 0.1),
     'L3_gnn_bk': (0.0, 0.1),
     'L3_gnn_bv': (0.0, 0.1),
     'L3_gnn_bo': (0.0, 0.1)}
    factors = {}
    for name, (base, spread) in spreads.items():
        noise = np.random.default_rng([zlib.crc32(name.encode()), seed]).standard_normal(out[name].shape)
        drawn = base * np.exp(spread * noise) if base else spread * noise
        out[name] = jnp.asarray(drawn.astype(out[name].dtype))
    for name, factor in factors.items():
        out[name] = (out[name] * factor).astype(out[name].dtype)
    return out
```

```python
from contextlib import ExitStack

import concourse.bass as bass
from concourse import mybir

F32 = mybir.dt.float32
F32R = mybir.dt.float32r
BF16 = mybir.dt.bfloat16
ALU = mybir.AluOpType
ACT = mybir.ActivationFunctionType
AX_X = mybir.AxisListType.X

P = 128
BANKS = 8
STREAMS = 2
LN_EPS = 1e-5
MASKED = 3e38
FAR = 1e9
GRU_STEPS = 3
LEAD = 3
T_RING, P_RING = 2, 4
SPARE = 32
HI, LO = 0, 1


class Signal:

    def __init__(self, sem, steps):
        self.sem, self.steps, self.next = sem, list(steps), 0

    def at(self, step, it):
        return it * len(self.steps) + self.steps.index(step) + 1

    def raised_by(self, instruction, step):
        assert self.steps[self.next] == step, (self.sem, self.steps[self.next], step)
        self.next = (self.next + 1) % len(self.steps)
        instruction.then_inc(self.sem, 1)


def attention_order(tiles, per_group):
    order = [("scores", t) for t in range(LEAD)]
    for t in range(tiles):
        if t + LEAD < tiles:
            order.append(("scores", t + LEAD))
        order.append(("transpose", t))
        if t % per_group == 2 and t >= per_group:
            order.append(("values", t // per_group - 1))
    order.append(("values", tiles // per_group - 1))
    return order


def adj_resnorm_kernel(nc, x, adj, w0, b0, wqkv, wproj, bproj, gamma, beta, w3, w3b, u3, u3b, w4, w4b,
                       w5, w5b, u5, u5b, wq, bq, wk, bk, wv, bv, wo, bo, out):
    B, N, D = x.shape
    H = 8
    HD = D // H
    NT = N // P
    FT = D // P
    HG = P // HD
    G = H // HG
    HALVES = 2
    QH = N // HALVES
    QT = QH // P
    PASSES = B // STREAMS
    SCALE = float(HD) ** -0.5
    GROUP = HG * QT
    GROUPS = G * HALVES
    TILES = GROUPS * GROUP
    ORDER = attention_order(STREAMS * TILES, GROUP)
    js = range(STREAMS)

    use = {}

    def take(*name):
        use[name] = len(use)

    def both(name, n):
        for j in js:
            for i in range(n):
                take(name, j, i)

    def attention_banks(layer):
        for what, t in ORDER:
            take(what, layer, t)

    both("ax", FT), both("w0", NT // 2), both("x1T", FT)
    for layer in (1, 3):
        for j in js:
            for kind in "qk":
                for g in range(G):
                    take(kind, layer, j, g)
            for tp in range(NT // 2):
                take("v", layer, j, tp)
        attention_banks(layer)
        both(f"proj{layer}", NT // 2)
        if layer == 1:
            both("x2T", FT)
            for s in range(GRU_STEPS):
                both(f"a{s}", FT)
                for j in js:
                    for kind in ("z", "r", "c"):
                        for o in range(FT):
                            take(f"{kind}{s}", j, o)
                both(f"h{s}", NT // 2)
            both("x3T", FT)
    SKIP = (4 - len(use) % 4) % 4
    on_bank = [[n for n, k in use.items() if (k + SKIP * (k >= BANKS)) % BANKS == i] for i in range(BANKS)]
    bank_of = {n: i for i in range(BANKS) for n in on_bank[i]}

    col, at = {}, 0
    for name in ("w0", "q1", "k1", "v1", "o1", "q3", "k3", "v3", "o3", "w3", "w4", "w5", "u3", "u5"):
        col[name] = at
        at += D
    WC = at
    PLAIN = col["w3"]

    x_v = x.rearrange("b (t p) d -> b p t d", p=P)
    out_v = out.rearrange("b (t p) d -> b p t d", p=P)

    with ExitStack() as ctx:
        def sb(name, shape, dt=F32):
            return ctx.enter_context(nc.sbuf_tensor(name, shape, dt))

        def sem(name):
            return ctx.enter_context(nc.semaphore(name))

        bank = [ctx.enter_context(nc.psum_tensor(f"bank{i}", [P, 512], F32)) for i in range(BANKS)]

        W = sb("W", [P, 2, FT, WC], F32R)
        adjT = sb("adjT", [P, 2, NT, N], F32R)
        mask1 = sb("mask1", [P, NT, N], BF16)
        mask3 = sb("mask3", [P, NT, N])
        rows = sb("rows", [P, 6, D])
        cols = sb("cols", [P, 7, FT])
        ident = sb("ident", [P, P])
        dinv = sb("dinv", [P, 3, NT])
        power = sb("power", [P, NT])
        eps = sb("eps", [P, NT])
        spare = sb("spare", [P, SPARE])
        res = [sb(f"res{j}", [P, NT, D]) for j in js]
        vh = [sb(f"vh{j}", [P, NT * D]) for j in js]
        feat = [sb(f"feat{j}", [P, 2, FT, N], F32R) for j in js]
        qn = [sb(f"qn{j}", [P, 2, 2 * N], F32R) for j in js]
        ka = [sb(f"ka{j}", [P, 2, FT, N], F32R) for j in js]
        stats = [sb(f"stats{j}", [P, NT, 6]) for j in js]
        mv = [sb(f"mv{j}", [P, NT, 2]) for j in js]
        rstd = [sb(f"rstd{j}", [P, NT]) for j in js]
        PT = sb("PT", [P, 2 * HG * NT * QH])
        T = sb("T", [P, T_RING, N])
        probs = sb("probs", [P, P_RING, N])
        least = sb("least", [P, P_RING])
        sums = sb("sums", [P, 2, QT * HG])
        rsum = sb("rsum", [P, 2, QT, HG * HD])
        rb = sb("rb", [P, 2, QH])
        o32 = sb("o32", [P, 2, QH])

        pt_v = PT[:, :].rearrange("p (b h k q) -> p b h k q", b=2, h=HG, k=NT)
        v_v = [vh[j][:, :].rearrange("p (t d) -> p t d", t=NT) for j in js]
        h_v = [vh[j][:, :].rearrange("p (f n) -> p f n", f=FT) for j in js]
        nat = [qn[j][:, :, :].rearrange("p s (t d) -> p s t d", t=NT) for j in js]
        q_v = [qn[j][:, :, :].rearrange("p s (g n) -> p s g n", g=G) for j in js]
        tmp = [[PT[:, (3 * j + i) * FT * N:(3 * j + i + 1) * FT * N].rearrange("p (f n) -> p f n", f=FT)
                for i in range(3)] for j in js]
        tz = [tmp[j][0] for j in js]
        tr = [tmp[j][1] for j in js]
        hv = [tmp[j][2] for j in js]
        raw = PT[:, 0:FT * PLAIN].rearrange("p (k c) -> p k c", k=FT)
        raw_w = [PT[:, FT * PLAIN + i * FT * 2 * D:FT * PLAIN + (i + 1) * FT * 2 * D]
                 .rearrange("p (o c) -> p o c", o=FT) for i in range(3)]
        raw_u = [res[1][:, 0:FT, :], res[1][:, FT:2 * FT, :]]
        adj_n = probs

        def wide(r, n):
            return rows[:, r:r + 1, :].broadcast_to([P, n, D])

        full = [sem(f"bank{i}_full") for i in range(BANKS)]
        x_loaded = [sem(f"x_loaded{j}") for j in js]
        stored = [sem(f"stored{j}") for j in js]
        raw_loaded = sem("raw_loaded")
        prep_pool = sem("prep_pool")
        prep_dve = sem("prep_dve")
        prep_act = sem("prep_act")
        prep_pe = sem("prep_pe")
        dve_mark = sem("dve_mark")

        steps_h = [f"h{s}{i}" for s in range(GRU_STEPS - 1) for i in range(2)]
        nat_steps = [f"x{t}" for t in range(NT)] + ["rows2"] + steps_h
        feat_steps = [f"ax{f}" for f in range(FT)] + [f"x1{f}" for f in range(FT)]
        feat_steps += [f"o1{g}" for g in range(GROUPS)] + [f"x2{f}" for f in range(FT)]
        lo_steps = feat_steps + [f"x3{f}" for f in range(FT)] + [f"o3{g}" for g in range(GROUPS)]
        for s in range(GRU_STEPS):
            feat_steps += [f"r{s}{f}" for f in range(FT)]
            if s < GRU_STEPS - 1:
                feat_steps += [f"h{s}{f}" for f in range(FT)]
        hi_steps = feat_steps + [f"x3{f}" for f in range(FT)] + [f"o3{g}" for g in range(GROUPS)]
        gru_steps = [f"{c}{s}{f}" for s in range(GRU_STEPS) for c in "rh"
                     if c == "r" or s < GRU_STEPS - 1 for f in range(FT)]
        qk_steps = {n: [f"{x}{n}{g}" for x in "qk" for g in range(G)] for n in (1, 3)}
        a_steps = [f"a{s}{f}" for s in range(GRU_STEPS) for f in range(FT)]
        norms = ["n0", "no", "n1", "n2", "n3"]
        pairs = [f"{n}{tp}" for n in norms for tp in range(NT // 2)]

        def signals(name, steps):
            return [Signal(sem(f"{name}{j}"), steps) for j in js]

        nat_hi = signals("nat_hi", nat_steps)
        nat_lo = signals("nat_lo", nat_steps)
        feat_hi = signals("feat_hi", hi_steps)
        feat_lo = signals("feat_lo", lo_steps)
        gru_lo = signals("gru_lo", gru_steps)
        qk_hi = signals("qk_hi", qk_steps[1] + a_steps + qk_steps[3])
        qk_lo = signals("qk_lo", qk_steps[1] + a_steps + qk_steps[3])
        v_ready = signals("v_ready", [f"v{n}{tp}" for n in (1, 3) for tp in range(NT // 2)])
        o_ready = signals("o_ready", [f"o{tp}" for tp in range(NT // 2)])
        var_ready = signals("var_ready", pairs)
        rstd_ready = signals("rstd_ready", pairs)
        var_eps = signals("var_eps", pairs)
        norm_ready = signals("norm_ready", [f"{n}{t}" for n in norms if n != "no" for t in range(NT)])
        biased = signals("biased", ["b0", "beta", "o0", "o1", "bo"])
        state = signals("state", ["x2_0", "x2_1"])
        gate_r = signals("gate_r", [f"r{s}{f}" for s in range(GRU_STEPS) for f in range(FT)])
        gate_z = signals("gate_z", [f"z{s}{f}" for s in range(GRU_STEPS) for f in range(FT)])
        cand = signals("cand", [f"c{s}{f}" for s in range(GRU_STEPS) for f in range(FT)])
        diff = signals("diff", [f"d{s}{f}" for s in range(GRU_STEPS) for f in range(FT)])
        reset = signals("reset", [f"r{s}{f}" for s in range(GRU_STEPS) for f in range(FT)])
        new_h = signals("new_h", [f"h{s}{f}" for s in range(GRU_STEPS) for f in range(FT)])
        tiles_all = [f"{n}.{t}" for n in (1, 3) for t in range(STREAMS * TILES)]
        groups_all = [f"{n}.{g}" for n in (1, 3) for g in range(STREAMS * GROUPS)]
        summed = signals("summed", [f"{n}{t}" for n in ("n0", "n1", "n2", "n3") for t in range(NT)])
        shifted = Signal(sem("shifted"), tiles_all)
        exped = Signal(sem("exped"), tiles_all)
        pt_act = Signal(sem("pt_act"), [f"{n}.{t}" for n in (1, 3) for t in range(0, STREAMS * TILES, 2)])
        pt_dve = Signal(sem("pt_dve"), [f"{n}.{t}" for n in (1, 3) for t in range(1, STREAMS * TILES, 2)])
        rsum_ready = Signal(sem("rsum_ready"), groups_all)
        rb_ready = Signal(sem("rb_ready"), groups_all)
        o32_ready = Signal(sem("o32_ready"), groups_all)

        def last_read(kind, *at):
            if kind in ("ax", "x1T", "x2T", "x3T"):
                return feat_lo[at[0]], f"{kind[:2]}{at[1]}"
            if kind in ("q", "k"):
                return qk_lo[at[1]], f"{kind}{at[0]}{at[2]}"
            if kind == "v":
                return v_ready[at[1]], f"v{at[0]}{at[2]}"
            if kind == "scores":
                return shifted, f"{at[0]}.{at[1]}"
            if kind == "transpose":
                return (pt_dve if at[1] % 2 else pt_act), f"{at[0]}.{at[1]}"
            if kind == "values":
                return o32_ready, f"{at[0]}.{at[1]}"
            if kind == "w0":
                return summed[at[0]], f"n0{2 * at[1] + 1}"
            if kind == "proj1":
                return o_ready[at[0]], f"o{at[1]}"
            if kind == "proj3":
                return summed[at[0]], f"n3{2 * at[1] + 1}"
            if kind == f"h{GRU_STEPS - 1}":
                return summed[at[0]], f"n2{2 * at[1] + 1}"
            of = {"a": qk_lo, "z": gate_z, "r": gate_r, "c": cand, "h": nat_lo}[kind[0]]
            return of[at[0]], f"{kind}{at[1]}"

        def place(*name):
            return bank[bank_of[name]]

        def wait_free(pe, it, *name):
            uses = on_bank[bank_of[name]]
            n = uses.index(name)
            if n:
                sig, step = last_read(*uses[n - 1])
                pe.wait_ge(sig.sem, sig.at(step, it))

        def fill(instruction, *name):
            instruction.then_inc(full[bank_of[name]], 1)

        def wait_full(eng, it, *name):
            uses = on_bank[bank_of[name]]
            eng.wait_ge(full[bank_of[name]], it * len(uses) + uses.index(name) + 1)

        def tile_of(t):
            j, r = divmod(t, TILES)
            gh, r = divmod(r, GROUP)
            h, q = divmod(r, QT)
            return j, gh // HALVES, gh % HALVES, h, q

        block = ctx.enter_context(nc.Block())

        RAW_LOADS = 16 * (1 + 3 + 2 + 7 + 6 + 7)
        PREP_SPLIT = 18
        PREP_DVE = PREP_SPLIT + NT + 5
        DVE_MARKS = STREAMS * (5 * NT + NT + GRU_STEPS * FT)

        @block.sync
        def _(sp):
            def raw_load(dst, src, **how):
                sp.dma_start(dst, src, **how).then_inc(raw_loaded, 16)

            raw_load(adj_n[:, :, :], adj.rearrange("(t p) m -> p t m", p=P))
            for i, w in enumerate((w3, w4, w5)):
                raw_load(raw_w[i], w.rearrange("(o p) c -> p o c", p=P))
            for i, w in enumerate((u3, u5)):
                raw_load(raw_u[i], w.rearrange("(o p) c -> p o c", p=P))
            for name, w in (("w0", w0), ("q1", wqkv), ("o1", wproj), ("q3", wq), ("k3", wk), ("v3", wv), ("o3", wo)):
                c = col[name]
                raw_load(raw[:, :, c:c + w.shape[1]], w.rearrange("(k p) c -> p k c", p=P))
            for i, b in enumerate((b0, bproj, gamma, beta, bv, bo)):
                raw_load(rows[:, i, :], b.partition_broadcast(P))
            for i, b in enumerate((bq, bk, w3b, u3b, w4b, w5b, u5b)):
                raw_load(cols[:, i, :], b.rearrange("(f p) -> p f", p=P),
                         allow_slow_non_contiguous=True)
            sp.wait_ge(prep_dve, PREP_DVE)
            def load(j, it):
                sp.dma_start(res[j][:, :, :], x_v[it * STREAMS + j]).then_inc(x_loaded[j], 16)

            def store(j, it):
                sp.wait_ge(norm_ready[j].sem, norm_ready[j].at(f"n3{NT - 1}", it))
                sp.dma_start(out_v[it * STREAMS + j], res[j][:, :, :]).then_inc(stored[j], 16)

            for j in js:
                load(j, 0)
            with sp.Fori(1, PASSES) as it:
                for j in js:
                    store(j, it - 1)
                    sp.wait_ge(stored[j], it * 16)
                    load(j, it)
            for j in js:
                store(j, PASSES - 1)
            for j in js:
                sp.wait_ge(stored[j], PASSES * 16)


        @block.gpsimd
        def _(pool):
            pool.memset(ident[:, :], 0.0).then_inc(prep_pool, 1)
            pool.memset(power[:, :], -0.5).then_inc(prep_pool, 1)
            pool.memset(eps[:, :], LN_EPS).then_inc(prep_pool, 1)
            pool.wait_ge(prep_pool, 3)
            pool.affine_select(out=ident[:, :], in_=ident[:, :], compare_op=ALU.not_equal, fill=1.0, base=0,
                               pattern=[[-1, P]], channel_multiplier=1).then_inc(prep_pool, 1)
            pool.wait_ge(prep_dve, 3)
            pool.tensor_tensor(dinv[:, 2, :], dinv[:, 1, :], power[:, :], ALU.pow).then_inc(prep_pool, 1)

            def rstds(j, tag, it):
                for tp in range(NT // 2):
                    step = f"{tag}{tp}"
                    sl = slice(2 * tp, 2 * tp + 2)
                    pool.wait_ge(var_ready[j].sem, var_ready[j].at(step, it))
                    i = pool.tensor_tensor(rstd[j][:, sl], mv[j][:, sl, 1], eps[:, sl], ALU.add)
                    var_eps[j].raised_by(i, step)
                    pool.wait_ge(var_eps[j].sem, var_eps[j].at(step, it))
                    i = pool.tensor_tensor(rstd[j][:, sl], rstd[j][:, sl], power[:, sl], ALU.pow)
                    rstd_ready[j].raised_by(i, step)

            with pool.Fori(0, PASSES) as it:
                for j in js:
                    pool.wait_ge(nat_lo[j].sem, nat_lo[j].at(f"x{NT - 1}", it))
                    i = pool.tensor_tensor(res[j][:, :, :], res[j][:, :, :], wide(0, NT), ALU.add)
                    biased[j].raised_by(i, "b0")
                for j in js:
                    rstds(j, "n0", it)
                for j in js:
                    pool.wait_ge(feat_lo[j].sem, feat_lo[j].at(f"x1{FT - 1}", it))
                    i = pool.tensor_tensor(res[j][:, :, :], res[j][:, :, :], wide(3, NT), ALU.add)
                    biased[j].raised_by(i, "beta")
                for j in js:
                    for tp in range(NT // 2):
                        sl = slice(2 * tp, 2 * tp + 2)
                        pool.wait_ge(o_ready[j].sem, o_ready[j].at(f"o{tp}", it))
                        pool.wait_ge(biased[j].sem, biased[j].at("beta", it))
                        i = pool.tensor_tensor(res[j][:, sl, :], res[j][:, sl, :], v_v[j][:, sl, :], ALU.add)
                        biased[j].raised_by(i, f"o{tp}")
                    rstds(j, "no", it)
                    rstds(j, "n1", it)
                for s in range(GRU_STEPS):
                    for j in js:
                        for f in range(FT):
                            pool.wait_ge(feat_hi[j].sem, feat_hi[j].at(f"r{s}{f}", it))
                            i = pool.tensor_tensor(feat[j][:, LO, f, :], tr[j][:, f, :],
                                                   feat[j][:, HI, f, :].bitcast(F32), ALU.subtract)
                            gru_lo[j].raised_by(i, f"r{s}{f}")
                    for j in js:
                        for f in range(FT):
                            pool.wait_ge(cand[j].sem, cand[j].at(f"c{s}{f}", it))
                            i = pool.tensor_tensor(hv[j][:, f, :], hv[j][:, f, :], h_v[j][:, f, :], ALU.subtract)
                            diff[j].raised_by(i, f"d{s}{f}")
                        if s < GRU_STEPS - 1:
                            for f in range(FT):
                                pool.wait_ge(feat_hi[j].sem, feat_hi[j].at(f"h{s}{f}", it))
                                i = pool.tensor_tensor(feat[j][:, LO, f, :], h_v[j][:, f, :],
                                                       feat[j][:, HI, f, :].bitcast(F32), ALU.subtract)
                                gru_lo[j].raised_by(i, f"h{s}{f}")
                for j in js:
                    rstds(j, "n2", it)
                for j in js:
                    pool.wait_ge(feat_lo[j].sem, feat_lo[j].at(f"x3{FT - 1}", it))
                    i = pool.tensor_tensor(res[j][:, :, :], res[j][:, :, :], wide(5, NT), ALU.add)
                    biased[j].raised_by(i, "bo")
                for j in js:
                    rstds(j, "n3", it)

        @block.scalar
        def _(act):
            act.wait_ge(prep_dve, 5)
            act.activation(W[:, HI, :, 0:PLAIN], raw, ACT.Copy).then_inc(prep_act, 1)
            for m in range(NT):
                act.wait_ge(prep_pe, m + 1)
                act.activation(adjT[:, HI, m, :], bank[m][:, :], ACT.Copy).then_inc(prep_act, 1)
            for i, name in enumerate(("w3", "w4", "w5", "u3", "u5")):
                act.wait_ge(prep_pe, NT + i + 1)
                c = col[name]
                act.activation(W[:, HI, :, c:c + D],
                               bank[(NT + i) % BANKS][:, :].rearrange("p (k c) -> p k c", k=FT),
                               ACT.Copy).then_inc(prep_act, 1)
            act.wait_ge(prep_dve, PREP_DVE)

            def evacuate_hi(j, it, name, steps, dst, bias=0.0):
                for i in range(2):
                    wait_full(act, it, *name, i)
                    b = bias if isinstance(bias, float) else bias[:, i:i + 1]
                    k = act.activation(dst(i), place(*name, i)[:, :], ACT.Identity, bias=b)
                    sig, step = steps(i)
                    sig.raised_by(k, step)

            def featured(j, it, name, tag):
                evacuate_hi(j, it, (name, j), lambda i: (feat_hi[j], f"{tag}{i}"), lambda i: feat[j][:, HI, i, :])

            def project_qkv(layer, it):
                for j in js:
                    for kind, dst in (("q", q_v[j]), ("k", ka[j])):
                        b = 0.0 if layer == 1 else cols[:, 0 if kind == "q" else 1, :]
                        evacuate_hi(j, it, (kind, layer, j), lambda i: (qk_hi[j], f"{kind}{layer}{i}"),
                                    lambda i: dst[:, HI, i, :], bias=b)

            def attention(layer, it):
                for what, t in ORDER:
                    if what == "scores":
                        j, g, half, h, q = tile_of(t)
                        grp = t // GROUP
                        act.wait_ge(shifted.sem, shifted.at(f"{layer}.{t}", it))
                        if t >= P_RING:
                            wait_full(act, it, "transpose", layer, t - P_RING)
                        k = act.activation(probs[:, t % P_RING, :], T[:, t % T_RING, :], ACT.Exp,
                                           bias=least[:, t % P_RING:t % P_RING + 1], scale=-1.0,
                                           accum_out=sums[:, grp % 2, q * HG + h:q * HG + h + 1])
                        exped.raised_by(k, f"{layer}.{t}")
                    elif what == "transpose" and t % 2 == 0:
                        move_pt(act, layer, t, it)
                    elif what == "values":
                        wait_full(act, it, "values", layer, t)
                        k = act.activation(rb[:, t % 2, :], place("values", layer, t)[:, QH:2 * QH], ACT.Copy)
                        rb_ready.raised_by(k, f"{layer}.{t}")
                        j, gh = divmod(t, GROUPS)
                        act.wait_ge(o32_ready.sem, o32_ready.at(f"{layer}.{t}", it))
                        half = gh % HALVES
                        k = act.activation(feat[j][:, HI, gh // HALVES, half * QH:(half + 1) * QH], o32[:, t % 2, :],
                                           ACT.Copy)
                        feat_hi[j].raised_by(k, f"o{layer}{gh}")

            def move_pt(eng, layer, t, it):
                j, g, half, h, q = tile_of(t)
                grp = t // GROUP
                wait_full(eng, it, "transpose", layer, t)
                if grp >= 2:
                    wait_full(eng, it, "values", layer, grp - 2)
                dst = pt_v[:, grp % 2, h, :, q * P:(q + 1) * P]
                src = place("transpose", layer, t)[:, :].rearrange("p (k q) -> p k q", k=NT)
                k = eng.activation(dst, src, ACT.Copy)
                pt_act.raised_by(k, f"{layer}.{t}")

            with act.Fori(0, PASSES) as it:
                for j in js:
                    act.wait_ge(x_loaded[j], it * 16 + 16)
                    for t in range(NT):
                        k = act.activation(nat[j][:, HI, t, :], res[j][:, t, :], ACT.Copy, scale=dinv[:, 0, t:t + 1])
                        nat_hi[j].raised_by(k, f"x{t}")
                for j in js:
                    featured(j, it, "ax", "ax")
                for j in js:
                    featured(j, it, "x1T", "x1")
                project_qkv(1, it)
                attention(1, it)
                for j in js:
                    for f in range(FT):
                        wait_full(act, it, "x2T", j, f)
                        k = act.activation(h_v[j][:, f, :], place("x2T", j, f)[:, :], ACT.Copy)
                        state[j].raised_by(k, f"x2_{f}")
                        k = act.activation(feat[j][:, HI, f, :], place("x2T", j, f)[:, :], ACT.Copy)
                        feat_hi[j].raised_by(k, f"x2{f}")
                    k = act.activation(nat[j][:, HI, :, :], res[j][:, :, :], ACT.Copy)
                    nat_hi[j].raised_by(k, "rows2")
                for s in range(GRU_STEPS):
                    for j in js:
                        evacuate_hi(j, it, (f"a{s}", j), lambda i: (qk_hi[j], f"a{s}{i}"), lambda i: ka[j][:, HI, i, :])
                    for j in js:
                        for f in range(FT):
                            wait_full(act, it, f"r{s}", j, f)
                            k = act.activation(tr[j][:, f, :], place(f"r{s}", j, f)[:, :], ACT.Tanh,
                                               bias=cols[:, 4, f:f + 1], scale=0.5)
                            gate_r[j].raised_by(k, f"r{s}{f}")
                        for f in range(FT):
                            wait_full(act, it, f"z{s}", j, f)
                            k = act.activation(tz[j][:, f, :], place(f"z{s}", j, f)[:, :], ACT.Tanh,
                                               bias=cols[:, 2, f:f + 1], scale=0.5)
                            gate_z[j].raised_by(k, f"z{s}{f}")
                        for f in range(FT):
                            act.wait_ge(reset[j].sem, reset[j].at(f"r{s}{f}", it))
                            k = act.activation(feat[j][:, HI, f, :], tr[j][:, f, :], ACT.Copy)
                            feat_hi[j].raised_by(k, f"r{s}{f}")
                    for j in js:
                        for f in range(FT):
                            wait_full(act, it, f"c{s}", j, f)
                            k = act.activation(hv[j][:, f, :], place(f"c{s}", j, f)[:, :], ACT.Tanh,
                                               bias=cols[:, 5, f:f + 1])
                            cand[j].raised_by(k, f"c{s}{f}")
                        if s < GRU_STEPS - 1:
                            for f in range(FT):
                                act.wait_ge(new_h[j].sem, new_h[j].at(f"h{s}{f}", it))
                                k = act.activation(feat[j][:, HI, f, :], h_v[j][:, f, :], ACT.Copy)
                                feat_hi[j].raised_by(k, f"h{s}{f}")
                    if s < GRU_STEPS - 1:
                        for j in js:
                            for tp in range(NT // 2):
                                wait_full(act, it, f"h{s}", j, tp)
                                k = act.activation(nat[j][:, HI, 2 * tp:2 * tp + 2, :],
                                                   place(f"h{s}", j, tp)[:, :].rearrange("p (t d) -> p t d", t=2),
                                                   ACT.Copy)
                                nat_hi[j].raised_by(k, f"h{s}{tp}")
                for j in js:
                    featured(j, it, "x3T", "x3")
                project_qkv(3, it)
                attention(3, it)

        @block.vector
        def _(dve):
            def prep(instruction):
                instruction.then_inc(prep_dve, 1)

            dve.wait_ge(raw_loaded, RAW_LOADS)
            prep(dve.tensor_reduce(out=dinv[:, 0, :], in_=adj_n[:, :, :], axis=AX_X, op=ALU.add))
            dve.wait_ge(prep_dve, 1)
            prep(dve.tensor_scalar(dinv[:, 1, :], dinv[:, 0, :], 1e-37, None, ALU.max))
            prep(dve.tensor_scalar(dinv[:, 0, :], dinv[:, 0, :], 0.0, None, ALU.is_gt))
            for name in ("q1", "q3"):
                c = col[name]
                prep(dve.tensor_scalar(raw[:, :, c:c + D], raw[:, :, c:c + D], -SCALE, None, ALU.mult))
            for i in range(3):
                prep(dve.tensor_tensor(raw_w[i][:, :, 0:D], raw_w[i][:, :, 0:D], raw_w[i][:, :, D:2 * D], ALU.add))
            prep(dve.tensor_scalar(raw_u[1], raw_u[1], 0.5, None, ALU.mult))
            prep(dve.tensor_scalar(mask1[:, :, :], adj_n[:, :, :], 0.0, MASKED, ALU.is_equal, ALU.mult))
            prep(dve.tensor_scalar(mask3[:, :, :], adj_n[:, :, :], 1.0, -FAR, ALU.subtract, ALU.mult))
            prep(dve.tensor_scalar(cols[:, 0, :], cols[:, 0, :], -SCALE, None, ALU.mult))
            for a, b in ((2, 3), (4, 3), (5, 6)):
                prep(dve.tensor_tensor(cols[:, a, :], cols[:, a, :], cols[:, b, :], ALU.add))
            dve.wait_ge(prep_dve, 15)
            prep(dve.tensor_scalar(cols[:, 2:5:2, :], cols[:, 2:5:2, :], 0.5, None, ALU.mult))
            dve.wait_ge(prep_pool, 5)
            prep(dve.tensor_tensor(dinv[:, 0, :], dinv[:, 0, :], dinv[:, 2, :], ALU.mult))
            dve.wait_ge(prep_act, 1)
            prep(dve.tensor_tensor(W[:, LO, :, 0:PLAIN], raw, W[:, HI, :, 0:PLAIN].bitcast(F32), ALU.subtract))
            for m in range(NT):
                dve.wait_ge(prep_act, 2 + m)
                prep(dve.tensor_tensor(adjT[:, LO, m, :], bank[m][:, :], adjT[:, HI, m, :].bitcast(F32),
                                       ALU.subtract))
            for i, name in enumerate(("w3", "w4", "w5", "u3", "u5")):
                dve.wait_ge(prep_act, 2 + NT + i)
                c = col[name]
                prep(dve.tensor_tensor(W[:, LO, :, c:c + D],
                                       bank[(NT + i) % BANKS][:, :].rearrange("p (k c) -> p k c", k=FT),
                                       W[:, HI, :, c:c + D].bitcast(F32), ALU.subtract))

            aparts = [0]

            def apart():
                aparts[0] = (aparts[0] + 1) % SPARE
                dve.memset(spare[:, aparts[0]:aparts[0] + 1], 0.0)

            marks = [0]

            def mark(instruction):
                marks[0] += 1
                instruction.then_inc(dve_mark, 1)
                return marks[0]

            def wait_mark(m, it):
                dve.wait_ge(dve_mark, it * DVE_MARKS + m)

            def evacuate_lo(j, it, name, steps, dst, hi, bias=None):
                for i in range(2):
                    hi_sig, lo_sig, step = steps(i)
                    dve.wait_ge(hi_sig.sem, hi_sig.at(step, it))
                    src = place(*name, i)[:, :]
                    if bias is None:
                        k = dve.tensor_tensor(dst(i), src, hi(i).bitcast(F32), ALU.subtract)
                    else:
                        k = dve.scalar_tensor_tensor(dst(i), src, bias[:, i:i + 1], hi(i).bitcast(F32),
                                                     ALU.add, ALU.subtract)
                    lo_sig.raised_by(k, step)

            def featured(j, it, name, tag):
                evacuate_lo(j, it, (name, j), lambda i: (feat_hi[j], feat_lo[j], f"{tag}{i}"),
                            lambda i: feat[j][:, LO, i, :], lambda i: feat[j][:, HI, i, :])

            def moments(j, it, tag, tp, src, written):
                ms = []
                for t in (2 * tp, 2 * tp + 1):
                    step = f"{tag}{t}" if written is not o_ready[j] else f"o{tp}"
                    dve.wait_ge(written.sem, written.at(step, it))
                    ms.append(mark(dve.bn_stats(stats[j][:, t, :], src[:, t, :])))
                for t, m in zip((2 * tp, 2 * tp + 1), ms):
                    wait_mark(m, it)
                    apart()
                    k = dve.bn_aggr(mv[j][:, t, :], stats[j][:, t, :])
                var_ready[j].raised_by(k, f"{tag}{tp}")

            def normalize(j, it, tag):
                for tp in range(NT // 2):
                    dve.wait_ge(rstd_ready[j].sem, rstd_ready[j].at(f"{tag}{tp}", it))
                    for t in (2 * tp, 2 * tp + 1):
                        k = dve.tensor_scalar(res[j][:, t, :], res[j][:, t, :], mv[j][:, t, 0:1],
                                              rstd[j][:, t:t + 1], ALU.subtract, ALU.mult)
                        norm_ready[j].raised_by(k, f"{tag}{t}")

            def project_qkv(layer, it):
                for j in js:
                    for kind, buf, r in (("q", q_v[j], 0), ("k", ka[j], 1)):
                        evacuate_lo(j, it, (kind, layer, j), lambda i: (qk_hi[j], qk_lo[j], f"{kind}{layer}{i}"),
                                    lambda i: buf[:, LO, i, :], lambda i: buf[:, HI, i, :],
                                    bias=None if layer == 1 else cols[:, r, :])
                    for tp in range(NT // 2):
                        wait_full(dve, it, "v", layer, j, tp)
                        src = place("v", layer, j, tp)[:, :].rearrange("p (t d) -> p t d", t=2)
                        dst = v_v[j][:, 2 * tp:2 * tp + 2, :]
                        if layer == 1:
                            k = dve.tensor_copy(dst, src)
                        else:
                            k = dve.tensor_tensor(dst, src, wide(4, 2), ALU.add)
                        v_ready[j].raised_by(k, f"v{layer}{tp}")

            def attention(layer, it):
                mask = mask1 if layer == 1 else mask3
                for what, t in ORDER:
                    if what == "scores":
                        j, g, half, h, q = tile_of(t)
                        wait_full(dve, it, "scores", layer, t)
                        if t >= T_RING:
                            dve.wait_ge(exped.sem, exped.at(f"{layer}.{t - T_RING}", it))
                        apart()
                        k = dve.tensor_tensor_reduce(
                            out=T[:, t % T_RING, :], in0=place("scores", layer, t)[:, :],
                            in1=mask[:, half * QT + q, :], scale=1.0, scalar=3.4e38, op0=ALU.add, op1=ALU.min,
                            accum_out=least[:, t % P_RING:t % P_RING + 1])
                        shifted.raised_by(k, f"{layer}.{t}")
                    elif what == "transpose":
                        j, g, half, h, q = tile_of(t)
                        grp = t // GROUP
                        if t % 2:
                            wait_full(dve, it, "transpose", layer, t)
                            if grp >= 2:
                                wait_full(dve, it, "values", layer, grp - 2)
                            k = dve.tensor_copy(pt_v[:, grp % 2, h, :, q * P:(q + 1) * P],
                                                place("transpose", layer, t)[:, :]
                                                .rearrange("p (k q) -> p k q", k=NT))
                            pt_dve.raised_by(k, f"{layer}.{t}")
                        if t % GROUP == GROUP - 1:
                            dve.wait_ge(exped.sem, exped.at(f"{layer}.{t}", it))
                            k = dve.reciprocal(rsum[:, grp % 2, :, :].rearrange("p q (h d) -> p (q h) d", h=HG),
                                               sums[:, grp % 2, :].unsqueeze(2).broadcast_to([P, QT * HG, HD]))
                            rsum_ready.raised_by(k, f"{layer}.{grp}")
                    else:
                        j, gh = divmod(t, GROUPS)
                        half = gh % HALVES
                        sl = slice(half * QH, (half + 1) * QH)
                        dve.wait_ge(rb_ready.sem, rb_ready.at(f"{layer}.{t}", it))
                        k = dve.tensor_tensor(o32[:, t % 2, :], place("values", layer, t)[:, 0:QH], rb[:, t % 2, :],
                                              ALU.mult)
                        o32_ready.raised_by(k, f"{layer}.{t}")
                        dve.wait_ge(feat_hi[j].sem, feat_hi[j].at(f"o{layer}{gh}", it))
                        k = dve.tensor_tensor(feat[j][:, LO, gh // HALVES, sl], o32[:, t % 2, :],
                                              feat[j][:, HI, gh // HALVES, sl].bitcast(F32), ALU.subtract)
                        feat_lo[j].raised_by(k, f"o{layer}{gh}")

            def residual(j, it, name, tag, after):
                dve.wait_ge(*after)
                for tp in range(NT // 2):
                    wait_full(dve, it, name, j, tp)
                    for i, t in enumerate((2 * tp, 2 * tp + 1)):
                        k = dve.tensor_tensor(res[j][:, t, :], place(name, j, tp)[:, i * D:(i + 1) * D],
                                              res[j][:, t, :], ALU.add)
                        summed[j].raised_by(k, f"{tag}{t}")
                    moments(j, it, tag, tp, res[j], summed[j])

            with dve.Fori(0, PASSES) as it:
                for j in js:
                    for t in range(NT):
                        dve.wait_ge(nat_hi[j].sem, nat_hi[j].at(f"x{t}", it))
                        k = dve.scalar_tensor_tensor(nat[j][:, LO, t, :], res[j][:, t, :], dinv[:, 0, t:t + 1],
                                                     nat[j][:, HI, t, :].bitcast(F32), ALU.mult, ALU.subtract)
                        nat_lo[j].raised_by(k, f"x{t}")
                for j in js:
                    featured(j, it, "ax", "ax")
                for j in js:
                    dve.wait_ge(biased[j].sem, biased[j].at("b0", it))
                    for tp in range(NT // 2):
                        wait_full(dve, it, "w0", j, tp)
                        for i, t in enumerate((2 * tp, 2 * tp + 1)):
                            k = dve.scalar_tensor_tensor(res[j][:, t, :], place("w0", j, tp)[:, i * D:(i + 1) * D],
                                                         dinv[:, 0, t:t + 1], res[j][:, t, :], ALU.mult, ALU.add)
                            summed[j].raised_by(k, f"n0{t}")
                        moments(j, it, "n0", tp, res[j], summed[j])
                    normalize(j, it, "n0")
                for j in js:
                    featured(j, it, "x1T", "x1")
                project_qkv(1, it)
                attention(1, it)
                for j in js:
                    for tp in range(NT // 2):
                        sl = slice(2 * tp, 2 * tp + 2)
                        wait_full(dve, it, "proj1", j, tp)
                        k = dve.tensor_tensor(v_v[j][:, sl, :],
                                              place("proj1", j, tp)[:, :].rearrange("p (t d) -> p t d", t=2),
                                              wide(1, 2), ALU.add)
                        o_ready[j].raised_by(k, f"o{tp}")
                    for tp in range(NT // 2):
                        moments(j, it, "no", tp, v_v[j], o_ready[j])
                    for tp in range(NT // 2):
                        dve.wait_ge(rstd_ready[j].sem, rstd_ready[j].at(f"no{tp}", it))
                        dve.wait_ge(biased[j].sem, biased[j].at(f"o{tp}", it))
                        ms = []
                        for t in (2 * tp, 2 * tp + 1):
                            ms.append(mark(dve.scalar_tensor_tensor(v_v[j][:, t, :], v_v[j][:, t, :],
                                                                    mv[j][:, t, 0:1], rows[:, 2, :],
                                                                    ALU.subtract, ALU.mult)))
                        for t, m in zip((2 * tp, 2 * tp + 1), ms):
                            wait_mark(m, it)
                            k = dve.scalar_tensor_tensor(res[j][:, t, :], v_v[j][:, t, :], rstd[j][:, t:t + 1],
                                                         res[j][:, t, :], ALU.mult, ALU.add)
                            summed[j].raised_by(k, f"n1{t}")
                        moments(j, it, "n1", tp, res[j], summed[j])
                    normalize(j, it, "n1")
                for j in js:
                    dve.wait_ge(nat_hi[j].sem, nat_hi[j].at("rows2", it))
                    k = dve.tensor_tensor(nat[j][:, LO, :, :], res[j][:, :, :], nat[j][:, HI, :, :].bitcast(F32),
                                          ALU.subtract)
                    nat_lo[j].raised_by(k, "rows2")
                    featured(j, it, "x2T", "x2")
                for s in range(GRU_STEPS):
                    for j in js:
                        evacuate_lo(j, it, (f"a{s}", j), lambda i: (qk_hi[j], qk_lo[j], f"a{s}{i}"),
                                    lambda i: ka[j][:, LO, i, :], lambda i: ka[j][:, HI, i, :])
                    for j in js:
                        for f in range(FT):
                            dve.wait_ge(gate_r[j].sem, gate_r[j].at(f"r{s}{f}", it))
                            k = dve.scalar_tensor_tensor(tr[j][:, f, :], tr[j][:, f, :], 1.0, h_v[j][:, f, :],
                                                         ALU.add, ALU.mult)
                            reset[j].raised_by(k, f"r{s}{f}")
                    for j in js:
                        ms = []
                        for f in range(FT):
                            dve.wait_ge(gate_z[j].sem, gate_z[j].at(f"z{s}{f}", it))
                            dve.wait_ge(diff[j].sem, diff[j].at(f"d{s}{f}", it))
                            ms.append(mark(dve.scalar_tensor_tensor(hv[j][:, f, :], tz[j][:, f, :], 1.0,
                                                                    hv[j][:, f, :], ALU.add, ALU.mult)))
                        for f in range(FT):
                            wait_mark(ms[f], it)
                            k = dve.scalar_tensor_tensor(h_v[j][:, f, :], hv[j][:, f, :], 0.5, h_v[j][:, f, :],
                                                         ALU.mult, ALU.add)
                            new_h[j].raised_by(k, f"h{s}{f}")
                    if s < GRU_STEPS - 1:
                        for j in js:
                            for tp in range(NT // 2):
                                dve.wait_ge(nat_hi[j].sem, nat_hi[j].at(f"h{s}{tp}", it))
                                sl = slice(2 * tp, 2 * tp + 2)
                                k = dve.tensor_tensor(nat[j][:, LO, sl, :],
                                                      place(f"h{s}", j, tp)[:, :].rearrange("p (t d) -> p t d", t=2),
                                                      nat[j][:, HI, sl, :].bitcast(F32), ALU.subtract)
                                nat_lo[j].raised_by(k, f"h{s}{tp}")
                for j in js:
                    residual(j, it, f"h{GRU_STEPS - 1}", "n2", (norm_ready[j].sem, norm_ready[j].at(f"n1{NT - 1}", it)))
                    normalize(j, it, "n2")
                for j in js:
                    featured(j, it, "x3T", "x3")
                project_qkv(3, it)
                attention(3, it)
                for j in js:
                    residual(j, it, "proj3", "n3", (biased[j].sem, biased[j].at("bo", it)))
                    normalize(j, it, "n3")
            assert marks[0] == DVE_MARKS, marks[0]

        @block.tensor
        def _(pe):
            pe.wait_ge(prep_pool, 4)
            pe.wait_ge(prep_dve, 11)
            for m in range(NT):
                for t in range(NT):
                    k = pe.transpose(bank[m][:, t * P:(t + 1) * P], adj_n[:, t, m * P:(m + 1) * P], ident[:, :])
                k.then_inc(prep_pe, 1)
            for i in range(5):
                w = raw_w[i] if i < 3 else raw_u[i - 3]
                b = NT + i
                if b >= BANKS:
                    pe.wait_ge(prep_dve, PREP_SPLIT + b - BANKS + 1)
                for kt in range(FT):
                    for o in range(FT):
                        k = pe.transpose(bank[b % BANKS][:, kt * D + o * P:kt * D + (o + 1) * P],
                                         w[:, o, kt * P:(kt + 1) * P], ident[:, :])
                k.then_inc(prep_pe, 1)
            pe.wait_ge(prep_dve, PREP_DVE)

            def product(dst, a, b, start, stop):
                pe.matmul(dst, a(HI), b(LO), start=start, stop=False)
                pe.matmul(dst, a(HI), b(HI), start=False, stop=False)
                return pe.matmul(dst, a(LO), b(HI), start=False, stop=stop)

            def wait_sig(sig, step, it):
                pe.wait_ge(sig.sem, sig.at(step, it))

            def weight(name, kt, o=None):
                c = col[name]
                if o is None:
                    return lambda s: W[:, s, kt, c:c + D]
                return lambda s: W[:, s, kt, c + o * P:c + (o + 1) * P]

            def adj_product(j, it, name, steps):
                for f in range(FT):
                    wait_free(pe, it, name, j, f)
                    for m in range(NT):
                        if f == 0:
                            for step in steps[m]:
                                wait_sig(nat_lo[j], step, it)
                        k = product(place(name, j, f)[:, :], lambda s: nat[j][:, s, m, f * P:(f + 1) * P],
                                    lambda s: adjT[:, s, m, :], m == 0, m == NT - 1)
                    fill(k, name, j, f)

            def row_product(it, name, src, w, waits):
                for tp in range(NT // 2):
                    wait_free(pe, it, *name, tp)
                    for sig, step in waits(tp):
                        wait_sig(sig, step, it)
                    for i in range(2):
                        t = 2 * tp + i
                        for kt in range(FT):
                            k = product(place(*name, tp)[:, i * D:(i + 1) * D],
                                        lambda s: src[:, s, kt, t * P:(t + 1) * P], weight(w, kt),
                                        kt == 0, kt == FT - 1)
                    fill(k, *name, tp)

            def col_product(dst, src, w, o, start, stop):
                for kt in range(FT):
                    k = product(dst, weight(w, kt, o), lambda s: src[:, s, kt, :], start and kt == 0,
                                stop and kt == FT - 1)
                return k

            def rows_to_features(j, it, name, tag):
                for f in range(FT):
                    wait_free(pe, it, name, j, f)
                    for t in range(NT):
                        if f == 0:
                            wait_sig(norm_ready[j], f"{tag}{t}", it)
                        k = pe.transpose(place(name, j, f)[:, t * P:(t + 1) * P], res[j][:, t, f * P:(f + 1) * P],
                                         ident[:, :])
                    fill(k, name, j, f)

            def project_qkv(layer, it):
                tag = "x1" if layer == 1 else "x3"
                for j in js:
                    wait_sig(feat_lo[j], f"{tag}{FT - 1}", it)
                    for kind in "qk":
                        for g in range(G):
                            wait_free(pe, it, kind, layer, j, g)
                            fill(col_product(place(kind, layer, j, g)[:, :], feat[j], f"{kind}{layer}", g, True, True),
                                 kind, layer, j, g)
                    row_product(it, ("v", layer, j), feat[j], f"v{layer}", lambda tp: ())

            def attention(layer, it):
                for what, t in ORDER:
                    wait_free(pe, it, what, layer, t)
                    dst = place(what, layer, t)
                    if what == "scores":
                        j, g, half, h, q = tile_of(t)
                        if t % TILES == 0:
                            wait_sig(qk_lo[j], f"k{layer}{G - 1}", it)
                        rs = slice(HD * h, HD * (h + 1))
                        cs = slice((half * QT + q) * P, (half * QT + q + 1) * P)
                        k = product(dst[:, :], lambda s: q_v[j][rs, s, g, cs], lambda s: ka[j][rs, s, g, :],
                                    True, True)
                    elif what == "transpose":
                        wait_sig(exped, f"{layer}.{t}", it)
                        for m in range(NT):
                            k = pe.transpose(dst[:, m * P:(m + 1) * P], probs[:, t % P_RING, m * P:(m + 1) * P],
                                             ident[:, :])
                    else:
                        j, gh = divmod(t, GROUPS)
                        g = gh // HALVES
                        last = (t + 1) * GROUP - 1
                        if gh == 0:
                            wait_sig(v_ready[j], f"v{layer}{NT // 2 - 1}", it)
                        wait_sig(rsum_ready, f"{layer}.{t}", it)
                        for q in range(QT):
                            pe.transpose(dst[:, QH + q * P:QH + (q + 1) * P], rsum[:, t % 2, q, :], ident[:, :])
                        wait_sig(pt_act, f"{layer}.{last - 1}", it)
                        wait_sig(pt_dve, f"{layer}.{last}", it)
                        for m in range(NT):
                            for h in range(HG):
                                c = (g * HG + h) * HD
                                k = pe.matmul(dst[h * HD:(h + 1) * HD, 0:QH], v_v[j][:, m, c:c + HD],
                                              pt_v[:, t % 2, h, m, :], start=(m == 0), stop=(m == NT - 1))
                    fill(k, what, layer, t)

            with pe.Fori(0, PASSES) as it:
                for j in js:
                    adj_product(j, it, "ax", [[f"x{t}"] for t in range(NT)])
                for j in js:
                    row_product(it, ("w0", j), feat[j], "w0",
                                lambda tp: [(feat_lo[j], f"ax{FT - 1}")] if tp == 0 else ())
                for j in js:
                    rows_to_features(j, it, "x1T", "n0")
                project_qkv(1, it)
                attention(1, it)
                for j in js:
                    row_product(it, ("proj1", j), feat[j], "o1",
                                lambda tp: [(feat_lo[j], f"o1{GROUPS - 2 + tp}")])
                for j in js:
                    rows_to_features(j, it, "x2T", "n1")
                for s in range(GRU_STEPS):
                    for j in js:
                        steps = [["rows2"]] + [[]] * (NT - 1) if s == 0 else \
                            [[f"h{s - 1}{t // 2}"] for t in range(NT)]
                        adj_product(j, it, f"a{s}", steps)
                    for j in js:
                        for kind in "zr":
                            for o in range(FT):
                                wait_free(pe, it, f"{kind}{s}", j, o)
                                if kind == "z" and o == 0:
                                    if s == 0:
                                        wait_sig(feat_lo[j], f"x2{FT - 1}", it)
                                    else:
                                        wait_sig(gru_lo[j], f"h{s - 1}{FT - 1}", it)
                                col_product(place(f"{kind}{s}", j, o)[:, :], feat[j], "u3", o, True, False)
                        wait_sig(qk_lo[j], f"a{s}{FT - 1}", it)
                        for kind, w in (("r", "w4"), ("z", "w3")):
                            for o in range(FT):
                                fill(col_product(place(f"{kind}{s}", j, o)[:, :], ka[j], w, o, False, True),
                                     f"{kind}{s}", j, o)
                        for o in range(FT):
                            wait_free(pe, it, f"c{s}", j, o)
                            col_product(place(f"c{s}", j, o)[:, :], ka[j], "w5", o, True, False)
                    for j in js:
                        wait_sig(gru_lo[j], f"r{s}{FT - 1}", it)
                        for o in range(FT):
                            fill(col_product(place(f"c{s}", j, o)[:, :], feat[j], "u5", o, False, True),
                                 f"c{s}", j, o)
                    for j in js:
                        for tp in range(NT // 2):
                            wait_free(pe, it, f"h{s}", j, tp)
                            for f in range(FT):
                                if tp == 0:
                                    wait_sig(new_h[j], f"h{s}{f}", it)
                                for i in range(2):
                                    t = 2 * tp + i
                                    k = pe.transpose(place(f"h{s}", j, tp)[:, i * D + f * P:i * D + (f + 1) * P],
                                                     h_v[j][:, f, t * P:(t + 1) * P], ident[:, :])
                            fill(k, f"h{s}", j, tp)
                for j in js:
                    rows_to_features(j, it, "x3T", "n2")
                project_qkv(3, it)
                attention(3, it)
                for j in js:
                    row_product(it, ("proj3", j), feat[j], "o3",
                                lambda tp: [(feat_lo[j], f"o3{GROUPS - 2 + tp}")])


_INS = ['x', 'adj', 'L0_gnn_weight', 'L0_gnn_bias', 'L1_gnn_w_qkv', 'L1_gnn_w_proj', 'L1_gnn_b_proj',
        'L1_gnn_ln_gamma', 'L1_gnn_ln_beta', 'L2_gnn_w3_w', 'L2_gnn_w3_b', 'L2_gnn_u3_w', 'L2_gnn_u3_b',
        'L2_gnn_w4_w', 'L2_gnn_w4_b', 'L2_gnn_w5_w', 'L2_gnn_w5_b', 'L2_gnn_u5_w', 'L2_gnn_u5_b', 'L3_gnn_Wq',
        'L3_gnn_bq', 'L3_gnn_Wk', 'L3_gnn_bk', 'L3_gnn_Wv', 'L3_gnn_bv', 'L3_gnn_Wo', 'L3_gnn_bo']


def kernel(**inputs):
    import numpy as _np
    import concourse.bacc as _bacc
    from concourse import mybir as _mybir
    from concourse.bass_utils import run_bass_kernel_spmd as _run

    nc = _bacc.Bacc("TRN2", target_bir_lowering=False, num_devices=1)
    arrays, args = {}, []
    for name in _INS:
        a = _np.ascontiguousarray(inputs[name])
        arrays[f"in_{name}_dram"] = a
        args.append(nc.dram_tensor(f"in_{name}_dram", a.shape, _mybir.dt.from_np(a.dtype), kind="ExternalInput").ap())
    shape = inputs["x"].shape
    args.append(nc.dram_tensor("out_dram", shape, _mybir.dt.float32, kind="ExternalOutput").ap())
    adj_resnorm_kernel(nc, *args)
    r = _run(nc, [arrays], core_ids=[0])
    return r.results[0]["out_dram"]
```

```python
from contextlib import ExitStack

import concourse.bass as bass
from concourse import mybir

F32 = mybir.dt.float32
F32R = mybir.dt.float32r
BF16 = mybir.dt.bfloat16
ALU = mybir.AluOpType
ACT = mybir.ActivationFunctionType
AX_X = mybir.AxisListType.X

P = 128
BANKS = 8
STREAMS = 2
LN_EPS = 1e-5
MASKED = 3e38
FAR = 1e9
GRU_STEPS = 3
LEAD = 3
P_RING = 4
SPARE = 32
HI, LO = 0, 1

PLAN = [
    [(('scale', 0), 0), (('ax', 0), 0), (('scale', 1), 0), (('w0', 0), 0), (('ax', 1), 0), (('norm0', 0), 0),
     (('x1T', 0), 0), (('w0', 1), 0), (('qkv', 1, 0), 0)],
    [(None, 0), (('norm0', 1), 2), (('x1T', 1), 3), (('qkv', 1, 1), 2)],
    [(None, 4), (('proj1', 0), 2), (('norm_o', 0), 2), (('norm1', 0), 2), (('x2T', 0), 3),
     (('adj_h', 0, 0), 3), (('gates', 0, 0), 3), (('update', 0, 0), 2), (('blend', 0, 0, 0), 2),
     (('blend', 0, 1, 0), 3)],
    [(('hT', 0, 0), 0), (('proj1', 1), 0), (('adj_h', 1, 0), 0), (('norm_o', 1), 0), (('gates', 1, 0), 0),
     (('norm1', 1), 0), (('update', 1, 0), 0), (('blend', 1, 0, 0), 0), (('blend', 1, 1, 0), 0),
     (('x2T', 1), 0), (('adj_h', 0, 1), 0), (('hT', 1, 0), 0), (('gates', 0, 1), 0), (('blend', 0, 0, 1), 0),
     (('adj_h', 2, 0), 0), (('update', 0, 1), 0), (('blend', 0, 1, 1), 0), (('gates', 2, 0), 0),
     (('hT', 0, 1), 0), (('update', 2, 0), 0), (('adj_h', 1, 1), 0), (('blend', 2, 0, 0), 0),
     (('blend', 2, 1, 0), 0), (('gates', 1, 1), 0), (('hT', 2, 0), 0), (('update', 1, 1), 0),
     (('norm2', 0), 0), (('x3T', 0), 0), (('blend', 1, 0, 1), 0), (('blend', 1, 1, 1), 0), (('qkv', 3, 0), 0),
     (('hT', 1, 1), 0)],
    [(None, 1), (('adj_h', 2, 1), 2), (('gates', 2, 1), 2), (('update', 2, 1), 1), (('blend', 2, 0, 1), 2),
     (('blend', 2, 1, 1), 2), (('hT', 2, 1), 4), (('norm2', 1), 3), (('x3T', 1), 3), (('qkv', 3, 1), 0)],
    [(None, 4), (('proj3', 0), 3), (('norm3', 0), 0)],
]


class Signal:
    ROUND = 16

    def __init__(self, sem, steps):
        self.sem, self.steps, self.next = sem, list(steps), 0
        self.total = -(-len(self.steps) // self.ROUND) * self.ROUND

    def value(self, i):
        return self.total if i == len(self.steps) - 1 else i + 1

    def at(self, step, it):
        return it * self.total + self.value(self.steps.index(step))

    def raised_by(self, instruction, step):
        i = self.next
        assert self.steps[i] == step, (self.sem, self.steps[i], step)
        instruction.then_inc(self.sem, self.value(i) - (self.value(i - 1) if i else 0))
        self.next = (i + 1) % len(self.steps)


def attention_step(layer, t, tiles, per_group):
    step = [("attend", layer, "scores", t + LEAD)] if t + LEAD < tiles else []
    step.append(("attend", layer, "transpose", t))
    if t % per_group == 2 and t >= per_group:
        step.append(("attend", layer, "values", t // per_group - 1))
    if t == tiles - 1:
        step.append(("attend", layer, "values", t // per_group))
    return step


def weave(steps, chain):
    out, n = [], 0
    for unit, follow in chain:
        if unit:
            out.append(unit)
        for step in steps[n:n + follow]:
            out += step
        n += follow
    for step in steps[n:]:
        out += step
    return out


def adj_resnorm_kernel(nc, x, adj, w0, b0, wqkv, wproj, bproj, gamma, beta, w3, w3b, u3, u3b, w4, w4b,
                       w5, w5b, u5, u5b, wq, bq, wk, bk, wv, bv, wo, bo, out):
    B, N, D = x.shape
    H = 8
    HD = D // H
    NT = N // P
    FT = D // P
    HG = P // HD
    G = H // HG
    HALVES = 2
    QH = N // HALVES
    QT = QH // P
    PASSES = B // STREAMS
    SCALE = float(HD) ** -0.5
    GROUP = HG * QT
    GROUPS = G * HALVES
    TILES = GROUPS * GROUP
    ALL = STREAMS * TILES
    js = range(STREAMS)

    steps = {n: [attention_step(n, t, ALL, GROUP) for t in range(ALL)] for n in (1, 3)}
    ahead = {n: [("attend", n, "scores", t) for t in range(LEAD)] for n in (1, 3)}
    before, first, second, between, third, fourth = PLAN
    SCHEDULE = [unit for unit, _ in before] + ahead[1] + weave(steps[1][:TILES], first)
    SCHEDULE += weave(steps[1][TILES:], second) + [unit for unit, _ in between] + ahead[3]
    SCHEDULE += weave(steps[3][:TILES], third) + weave(steps[3][TILES:], fourth)
    SCHEDULE += [("proj3", 1), ("norm3", 1)]

    on_bank = [[] for _ in range(BANKS)]
    bank_of, is_open, at = {}, set(), 0

    def take(*name):
        nonlocal at
        while at in is_open:
            at = (at + 1) % BANKS
        on_bank[at].append(name)
        bank_of[name] = at
        at = (at + 1) % BANKS

    for unit in SCHEDULE:
        kind, j = unit[0], unit[-1]
        if kind in ("ax", "x1T", "x2T", "x3T", "w0", "proj1", "proj3"):
            take(kind, j, 0), take(kind, j, 1)
        elif kind == "qkv":
            for what in "qkv":
                take(what, unit[1], j, 0), take(what, unit[1], j, 1)
        elif kind == "attend":
            take(unit[2], unit[1], unit[3])
        elif kind in ("adj_h", "hT"):
            what = f"{kind[0]}{unit[1]}"
            take(what, j, 0), take(what, j, 1)
        elif kind == "gates":
            for what in (f"z{unit[1]}", f"r{unit[1]}", f"c{unit[1]}"):
                take(what, j, 0), take(what, j, 1)
            is_open |= {bank_of[what, j, 0], bank_of[what, j, 1]}
        elif kind == "update":
            is_open -= {bank_of[f"c{unit[1]}", j, o] for o in range(2)}

    col, at = {}, 0
    for name in ("w0", "q1", "k1", "v1", "o1", "q3", "k3", "v3", "o3", "w3", "w4", "w5", "u3", "u5"):
        col[name] = at
        at += D
    WC = at
    PLAIN = col["w3"]

    x_v = x.rearrange("b (t p) d -> b p t d", p=P)
    out_v = out.rearrange("b (t p) d -> b p t d", p=P)

    with ExitStack() as ctx:
        def sb(name, shape, dt=F32):
            return ctx.enter_context(nc.sbuf_tensor(name, shape, dt))

        def sem(name):
            return ctx.enter_context(nc.semaphore(name))

        bank = [ctx.enter_context(nc.psum_tensor(f"bank{i}", [P, 512], F32)) for i in range(BANKS)]

        W = sb("W", [P, 2, FT, WC], F32R)
        adjT = sb("adjT", [P, 2, NT, N], F32R)
        mask1 = sb("mask1", [P, NT, N], BF16)
        mask3 = sb("mask3", [P, NT, N])
        rows = sb("rows", [P, 6, D])
        cols = sb("cols", [P, 7, FT])
        ident = sb("ident", [P, P])
        dinv = sb("dinv", [P, 3, NT])
        power = sb("power", [P, NT])
        eps = sb("eps", [P, NT])
        ones = sb("ones", [P, QT * HG])
        spare = sb("spare", [P, SPARE])
        res = [sb(f"res{j}", [P, NT, D]) for j in js]
        vh = [sb(f"vh{j}", [P, NT * D]) for j in js]
        feat = [sb(f"feat{j}", [P, 2, FT, N], F32R) for j in js]
        qn = [sb(f"qn{j}", [P, 2, 2 * N], F32R) for j in js]
        ka = [sb(f"ka{j}", [P, 2, FT, N], F32R) for j in js]
        stats = [sb(f"stats{j}", [P, NT, 6]) for j in js]
        mv = [sb(f"mv{j}", [P, NT, 2]) for j in js]
        rstd = [sb(f"rstd{j}", [P, NT]) for j in js]
        gate_z32 = sb("gate_z32", [P, FT, N])
        gate_t32 = sb("gate_t32", [P, FT, N])
        PT = sb("PT", [P, 2 * HG * NT * QH])
        probs = sb("probs", [P, P_RING, N])
        least = sb("least", [P, P_RING])
        sums = sb("sums", [P, 2, QT * HG])
        recip = sb("recip", [P, 2, QT * HG])
        rsum = sb("rsum", [P, QT, HG * HD])
        o32 = sb("o32", [P, 2, QH])

        pt_v = PT[:, :].rearrange("p (b h k q) -> p b h k q", b=2, h=HG, k=NT)
        v_v = [vh[j][:, :].rearrange("p (t d) -> p t d", t=NT) for j in js]
        h_v = [vh[j][:, :].rearrange("p (f n) -> p f n", f=FT) for j in js]
        nat = [qn[j][:, :, :].rearrange("p s (t d) -> p s t d", t=NT) for j in js]
        q_v = [qn[j][:, :, :].rearrange("p s (g n) -> p s g n", g=G) for j in js]
        in_PT = [PT[:, i * FT * N:(i + 1) * FT * N].rearrange("p (f n) -> p f n", f=FT) for i in range(2)]

        def tz(s, j):
            return in_PT[0] if (j == 1 and s < GRU_STEPS - 1) else gate_z32

        def tr(s, j):
            return in_PT[1] if (j == 1 and s < GRU_STEPS - 1) else gate_t32

        raw = PT[:, 0:FT * PLAIN].rearrange("p (k c) -> p k c", k=FT)
        raw_w = [PT[:, FT * PLAIN + i * FT * 2 * D:FT * PLAIN + (i + 1) * FT * 2 * D]
                 .rearrange("p (o c) -> p o c", o=FT) for i in range(3)]
        raw_u = [res[1][:, 0:FT, :], res[1][:, FT:2 * FT, :]]
        adj_n = probs

        def wide(r, n):
            return rows[:, r:r + 1, :].broadcast_to([P, n, D])

        full = [Signal(sem(f"bank{i}_full"), on_bank[i]) for i in range(BANKS)]
        x_loaded = [sem(f"x_loaded{j}") for j in js]
        stored = [sem(f"stored{j}") for j in js]
        adj_loaded = sem("adj_loaded")
        raw_loaded = sem("raw_loaded")
        prep_pool = sem("prep_pool")
        prep_dve = sem("prep_dve")
        prep_act = sem("prep_act")
        prep_pe = sem("prep_pe")
        dve_mark = sem("dve_mark")

        steps_h = [f"h{s}{i}" for s in range(GRU_STEPS - 1) for i in range(2)]
        nat_steps = [f"x{t}" for t in range(NT)] + ["rows2"] + steps_h
        feat_steps = [f"ax{f}" for f in range(FT)] + [f"x1{f}" for f in range(FT)]
        feat_steps += [f"o1{g}" for g in range(GROUPS)] + [f"x2{f}" for f in range(FT)]
        lo_steps = feat_steps + [f"x3{f}" for f in range(FT)] + [f"o3{g}" for g in range(GROUPS)]
        for s in range(GRU_STEPS):
            feat_steps += [f"r{s}{f}" for f in range(FT)]
            if s < GRU_STEPS - 1:
                feat_steps += [f"h{s}{f}" for f in range(FT)]
        hi_steps = feat_steps + [f"x3{f}" for f in range(FT)] + [f"o3{g}" for g in range(GROUPS)]
        gru_steps = [f"{c}{s}{f}" for s in range(GRU_STEPS) for c in "rh"
                     if c == "r" or s < GRU_STEPS - 1 for f in range(FT)]
        qk_steps = {n: [f"{x}{n}{g}" for x in "qk" for g in range(G)] for n in (1, 3)}
        a_steps = [f"a{s}{f}" for s in range(GRU_STEPS) for f in range(FT)]
        norms = ["n0", "no", "n1", "n2", "n3"]
        pairs = [f"{n}{tp}" for n in norms for tp in range(NT // 2)]

        def signals(name, steps):
            return [Signal(sem(f"{name}{j}"), steps) for j in js]

        nat_hi = signals("nat_hi", nat_steps)
        nat_lo = signals("nat_lo", nat_steps)
        feat_hi = signals("feat_hi", hi_steps)
        feat_lo = signals("feat_lo", lo_steps)
        gru_lo = signals("gru_lo", gru_steps)
        qk_hi = signals("qk_hi", qk_steps[1] + a_steps + qk_steps[3])
        qk_lo = signals("qk_lo", qk_steps[1] + a_steps + qk_steps[3])
        v_ready = signals("v_ready", [f"v{n}{tp}" for n in (1, 3) for tp in range(NT // 2)])
        o_ready = signals("o_ready", [f"o{tp}" for tp in range(NT // 2)])
        var_ready = signals("var_ready", pairs)
        rstd_ready = signals("rstd_ready", pairs)
        var_eps = signals("var_eps", pairs)
        norm_ready = signals("norm_ready", [f"{n}{t}" for n in norms if n != "no" for t in range(NT)])
        biased = signals("biased", ["b0", "beta", "bo"])
        state = signals("state", ["x2_0", "x2_1"])
        gate_r = signals("gate_r", [f"r{s}{f}" for s in range(GRU_STEPS) for f in range(FT)])
        gate_z = signals("gate_z", [f"z{s}{f}" for s in range(GRU_STEPS) for f in range(FT)])
        cand = signals("cand", [f"c{s}{f}" for s in range(GRU_STEPS) for f in range(FT)])
        reset = signals("reset", [f"r{s}{f}" for s in range(GRU_STEPS) for f in range(FT)])
        new_h = signals("new_h", [f"h{s}{f}" for s in range(GRU_STEPS) for f in range(FT)])
        tiles_all = [f"{n}.{t}" for n in (1, 3) for t in range(STREAMS * TILES)]
        groups_all = [f"{n}.{g}" for n in (1, 3) for g in range(STREAMS * GROUPS)]
        summed = signals("summed", [f"{n}{t}" for n in ("n0", "n1", "n2", "n3") for t in range(NT)])
        shifted = Signal(sem("shifted"), tiles_all)
        exped = Signal(sem("exped"), tiles_all)
        pt_act = Signal(sem("pt_act"), [f"{n}.{t}" for n in (1, 3) for t in range(0, STREAMS * TILES, 2)])
        pt_dve = Signal(sem("pt_dve"), [f"{n}.{t}" for n in (1, 3) for t in range(1, STREAMS * TILES, 2)])
        recip_ready = Signal(sem("recip_ready"), groups_all)
        rsum_ready = Signal(sem("rsum_ready"), groups_all)
        rb_ready = Signal(sem("rb_ready"), groups_all)
        o32_ready = Signal(sem("o32_ready"), groups_all)

        def last_read(kind, *at):
            if kind in ("ax", "x1T", "x2T", "x3T"):
                return feat_lo[at[0]], f"{kind[:2]}{at[1]}"
            if kind in ("q", "k"):
                return qk_lo[at[1]], f"{kind}{at[0]}{at[2]}"
            if kind == "v":
                return v_ready[at[1]], f"v{at[0]}{at[2]}"
            if kind == "scores":
                return shifted, f"{at[0]}.{at[1]}"
            if kind == "transpose":
                return (pt_dve if at[1] % 2 else pt_act), f"{at[0]}.{at[1]}"
            if kind == "values":
                return o32_ready, f"{at[0]}.{at[1]}"
            if kind == "w0":
                return summed[at[0]], f"n0{2 * at[1] + 1}"
            if kind == "proj1":
                return o_ready[at[0]], f"o{at[1]}"
            if kind == "proj3":
                return summed[at[0]], f"n3{2 * at[1] + 1}"
            if kind == f"h{GRU_STEPS - 1}":
                return summed[at[0]], f"n2{2 * at[1] + 1}"
            of = {"a": qk_lo, "z": gate_z, "r": gate_r, "c": cand, "h": nat_lo}[kind[0]]
            return of[at[0]], f"{kind}{at[1]}"

        def place(*name):
            return bank[bank_of[name]]

        def wait_free(pe, it, *name):
            uses = on_bank[bank_of[name]]
            n = uses.index(name)
            if n:
                sig, step = last_read(*uses[n - 1])
                pe.wait_ge(sig.sem, sig.at(step, it))

        def fill(instruction, *name):
            full[bank_of[name]].raised_by(instruction, name)

        def wait_full(eng, it, *name):
            bank_full = full[bank_of[name]]
            eng.wait_ge(bank_full.sem, bank_full.at(name, it))

        def tile_of(t):
            j, r = divmod(t, TILES)
            gh, r = divmod(r, GROUP)
            h, q = divmod(r, QT)
            return j, gh // HALVES, gh % HALVES, h, q

        block = ctx.enter_context(nc.Block())

        RAW_LOADS = 16 * (3 + 2 + 7 + 6 + 7)
        PREP_DVE = 18 + NT + 5
        DVE_MARKS = STREAMS * (5 * NT + NT + NT // 2 + GRU_STEPS * 2 * FT)

        @block.sync
        def _(sp):
            def raw_load(dst, src, **how):
                sp.dma_start(dst, src, **how).then_inc(raw_loaded, 16)

            sp.dma_start(adj_n[:, :, :], adj.rearrange("(t p) m -> p t m", p=P)).then_inc(adj_loaded, 16)
            for i, w in enumerate((w3, w4, w5)):
                raw_load(raw_w[i], w.rearrange("(o p) c -> p o c", p=P))
            for i, w in enumerate((u3, u5)):
                raw_load(raw_u[i], w.rearrange("(o p) c -> p o c", p=P))
            for name, w in (("w0", w0), ("q1", wqkv), ("o1", wproj), ("q3", wq), ("k3", wk), ("v3", wv), ("o3", wo)):
                c = col[name]
                raw_load(raw[:, :, c:c + w.shape[1]], w.rearrange("(k p) c -> p k c", p=P))
            for i, b in enumerate((b0, bproj, gamma, beta, bv, bo)):
                raw_load(rows[:, i, :], b.partition_broadcast(P))
            for i, b in enumerate((bq, bk, w3b, u3b, w4b, w5b, u5b)):
                raw_load(cols[:, i, :], b.rearrange("(f p) -> p f", p=P),
                         allow_slow_non_contiguous=True)
            sp.wait_ge(prep_dve, PREP_DVE)
            def load(j, it):
                sp.dma_start(res[j][:, :, :], x_v[it * STREAMS + j]).then_inc(x_loaded[j], 16)

            def store(j, it):
                sp.wait_ge(norm_ready[j].sem, norm_ready[j].at(f"n3{NT - 1}", it))
                sp.dma_start(out_v[it * STREAMS + j], res[j][:, :, :]).then_inc(stored[j], 16)

            for j in js:
                load(j, 0)
            with sp.Fori(1, PASSES) as it:
                for j in js:
                    store(j, it - 1)
                    sp.wait_ge(stored[j], it * 16)
                    load(j, it)
            for j in js:
                store(j, PASSES - 1)
            for j in js:
                sp.wait_ge(stored[j], PASSES * 16)


        @block.gpsimd
        def _(pool):
            pool.memset(ident[:, :], 0.0).then_inc(prep_pool, 1)
            pool.memset(power[:, :], -0.5).then_inc(prep_pool, 1)
            pool.memset(eps[:, :], LN_EPS).then_inc(prep_pool, 1)
            pool.memset(ones[:, :], 1.0).then_inc(prep_pool, 1)
            pool.wait_ge(prep_pool, 4)
            pool.affine_select(out=ident[:, :], in_=ident[:, :], compare_op=ALU.not_equal, fill=1.0, base=0,
                               pattern=[[-1, P]], channel_multiplier=1).then_inc(prep_pool, 1)
            pool.wait_ge(prep_dve, 3)
            pool.tensor_tensor(dinv[:, 2, :], dinv[:, 1, :], power[:, :], ALU.pow).then_inc(prep_pool, 1)

            def rstds(j, tag, it):
                for tp in range(NT // 2):
                    step = f"{tag}{tp}"
                    sl = slice(2 * tp, 2 * tp + 2)
                    pool.wait_ge(var_ready[j].sem, var_ready[j].at(step, it))
                    i = pool.tensor_tensor(rstd[j][:, sl], mv[j][:, sl, 1], eps[:, sl], ALU.add)
                    var_eps[j].raised_by(i, step)
                    pool.wait_ge(var_eps[j].sem, var_eps[j].at(step, it))
                    i = pool.tensor_tensor(rstd[j][:, sl], rstd[j][:, sl], power[:, sl], ALU.pow)
                    rstd_ready[j].raised_by(i, step)

            def scale(j, it):
                pool.wait_ge(nat_lo[j].sem, nat_lo[j].at(f"x{NT - 1}", it))
                i = pool.tensor_tensor(res[j][:, :, :], res[j][:, :, :], wide(0, NT), ALU.add)
                biased[j].raised_by(i, "b0")

            def qkv(layer, j, it):
                pool.wait_ge(feat_lo[j].sem, feat_lo[j].at(f"x{layer}{FT - 1}", it))
                i = pool.tensor_tensor(res[j][:, :, :], res[j][:, :, :], wide(3 if layer == 1 else 5, NT), ALU.add)
                biased[j].raised_by(i, "beta" if layer == 1 else "bo")

            def proj1(j, it):
                rstds(j, "no", it)
                rstds(j, "n1", it)

            def gates(s, j, it):
                for f in range(FT):
                    pool.wait_ge(feat_hi[j].sem, feat_hi[j].at(f"r{s}{f}", it))
                    i = pool.tensor_tensor(feat[j][:, LO, f, :], tr(s, j)[:, f, :],
                                           feat[j][:, HI, f, :].bitcast(F32), ALU.subtract)
                    gru_lo[j].raised_by(i, f"r{s}{f}")

            def hT(s, j, it):
                if s < GRU_STEPS - 1:
                    for f in range(FT):
                        pool.wait_ge(feat_hi[j].sem, feat_hi[j].at(f"h{s}{f}", it))
                        i = pool.tensor_tensor(feat[j][:, LO, f, :], h_v[j][:, f, :],
                                               feat[j][:, HI, f, :].bitcast(F32), ALU.subtract)
                        gru_lo[j].raised_by(i, f"h{s}{f}")
                else:
                    rstds(j, "n2", it)

            def attend(layer, what, t, it):
                if what == "transpose" and t % GROUP == GROUP - 1:
                    g = t // GROUP
                    pool.wait_ge(recip_ready.sem, recip_ready.at(f"{layer}.{g}", it))
                    if g:
                        wait_full(pool, it, "values", layer, g - 1)
                    i = pool.tensor_tensor(rsum[:, :, :].rearrange("p q (h d) -> p (q h) d", h=HG),
                                           recip[:, g % 2, :].unsqueeze(2).broadcast_to([P, QT * HG, HD]),
                                           ones[:, :].unsqueeze(2).broadcast_to([P, QT * HG, HD]), ALU.mult)
                    rsum_ready.raised_by(i, f"{layer}.{g}")

            with pool.Fori(0, PASSES) as it:
                for unit in SCHEDULE:
                    kind, args = unit[0], unit[1:]
                    if kind == "scale":
                        scale(*args, it)
                    elif kind == "w0":
                        rstds(*args, "n0", it)
                    elif kind == "qkv":
                        qkv(*args, it)
                    elif kind == "attend":
                        attend(*args, it)
                    elif kind == "proj1":
                        proj1(*args, it)
                    elif kind == "gates":
                        gates(*args, it)
                    elif kind == "hT":
                        hT(*args, it)
                    elif kind == "proj3":
                        rstds(*args, "n3", it)

        @block.scalar
        def _(act):
            for m in range(NT):
                act.wait_ge(prep_pe, m + 1)
                act.activation(adjT[:, HI, m, :], bank[m][:, :], ACT.Copy).then_inc(prep_act, 1)
            act.wait_ge(prep_dve, 7 + NT)
            act.activation(W[:, HI, :, 0:PLAIN], raw, ACT.Copy).then_inc(prep_act, 1)
            for i, name in enumerate(("w3", "w4", "w5", "u3", "u5")):
                act.wait_ge(prep_pe, NT + i + 1)
                c = col[name]
                act.activation(W[:, HI, :, c:c + D],
                               bank[(NT + i) % BANKS][:, :].rearrange("p (k c) -> p k c", k=FT),
                               ACT.Copy).then_inc(prep_act, 1)
            act.wait_ge(prep_dve, PREP_DVE)

            def evacuate_hi(j, it, name, steps, dst, bias=0.0):
                for i in range(2):
                    wait_full(act, it, *name, i)
                    b = bias if isinstance(bias, float) else bias[:, i:i + 1]
                    k = act.activation(dst(i), place(*name, i)[:, :], ACT.Identity, bias=b)
                    sig, step = steps(i)
                    sig.raised_by(k, step)

            def featured(j, it, name, tag):
                evacuate_hi(j, it, (name, j), lambda i: (feat_hi[j], f"{tag}{i}"), lambda i: feat[j][:, HI, i, :])

            def qkv(layer, j, it):
                for kind, dst in (("q", q_v[j]), ("k", ka[j])):
                    b = 0.0 if layer == 1 else cols[:, 0 if kind == "q" else 1, :]
                    evacuate_hi(j, it, (kind, layer, j), lambda i: (qk_hi[j], f"{kind}{layer}{i}"),
                                lambda i: dst[:, HI, i, :], bias=b)

            def attend(layer, what, t, it):
                if what == "scores":
                    j, g, half, h, q = tile_of(t)
                    grp = t // GROUP
                    act.wait_ge(shifted.sem, shifted.at(f"{layer}.{t}", it))
                    p = probs[:, t % P_RING, :]
                    k = act.activation(p, p, ACT.Exp, bias=least[:, t % P_RING:t % P_RING + 1], scale=-1.0,
                                       accum_out=sums[:, grp % 2, q * HG + h:q * HG + h + 1])
                    exped.raised_by(k, f"{layer}.{t}")
                elif what == "transpose":
                    if t % 2 == 0:
                        move_pt(act, layer, t, it)
                else:
                    j, gh = divmod(t, GROUPS)
                    sl = slice(gh % HALVES * QH, (gh % HALVES + 1) * QH)
                    wait_full(act, it, "values", layer, t)
                    k = act.activation(o32[:, t % 2, :], place("values", layer, t)[:, QH:2 * QH], ACT.Copy)
                    rb_ready.raised_by(k, f"{layer}.{t}")
                    act.wait_ge(o32_ready.sem, o32_ready.at(f"{layer}.{t}", it))
                    k = act.activation(feat[j][:, HI, gh // HALVES, sl], o32[:, t % 2, :], ACT.Copy)
                    feat_hi[j].raised_by(k, f"o{layer}{gh}")

            def move_pt(eng, layer, t, it):
                j, g, half, h, q = tile_of(t)
                grp = t // GROUP
                wait_full(eng, it, "transpose", layer, t)
                if grp >= 2:
                    wait_full(eng, it, "values", layer, grp - 2)
                dst = pt_v[:, grp % 2, h, :, q * P:(q + 1) * P]
                src = place("transpose", layer, t)[:, :].rearrange("p (k q) -> p k q", k=NT)
                k = eng.activation(dst, src, ACT.Copy)
                pt_act.raised_by(k, f"{layer}.{t}")

            def scale(j, it):
                act.wait_ge(x_loaded[j], it * 16 + 16)
                for t in range(NT):
                    k = act.activation(nat[j][:, HI, t, :], res[j][:, t, :], ACT.Copy, scale=dinv[:, 0, t:t + 1])
                    nat_hi[j].raised_by(k, f"x{t}")

            def x2T(j, it):
                for f in range(FT):
                    wait_full(act, it, "x2T", j, f)
                    k = act.activation(h_v[j][:, f, :], place("x2T", j, f)[:, :], ACT.Copy)
                    state[j].raised_by(k, f"x2_{f}")
                    k = act.activation(feat[j][:, HI, f, :], place("x2T", j, f)[:, :], ACT.Copy)
                    feat_hi[j].raised_by(k, f"x2{f}")
                k = act.activation(nat[j][:, HI, :, :], res[j][:, :, :], ACT.Copy)
                nat_hi[j].raised_by(k, "rows2")

            def gates(s, j, it):
                for kind, dst, c, sig in (("r", tr(s, j), 4, gate_r[j]), ("z", tz(s, j), 2, gate_z[j])):
                    for f in range(FT):
                        wait_full(act, it, f"{kind}{s}", j, f)
                        k = act.activation(dst[:, f, :], place(f"{kind}{s}", j, f)[:, :], ACT.Tanh,
                                           bias=cols[:, c, f:f + 1], scale=0.5)
                        sig.raised_by(k, f"{kind}{s}{f}")
                        if kind == "z":
                            act.wait_ge(reset[j].sem, reset[j].at(f"r{s}{f}", it))
                            k = act.activation(feat[j][:, HI, f, :], tr(s, j)[:, f, :], ACT.Copy)
                            feat_hi[j].raised_by(k, f"r{s}{f}")

            def update(s, j, it):
                for f in range(FT):
                    wait_full(act, it, f"c{s}", j, f)
                    k = act.activation(tr(s, j)[:, f, :], place(f"c{s}", j, f)[:, :], ACT.Tanh, bias=cols[:, 5, f:f + 1])
                    cand[j].raised_by(k, f"c{s}{f}")

            def hT(s, j, it):
                if s < GRU_STEPS - 1:
                    for tp in range(NT // 2):
                        wait_full(act, it, f"h{s}", j, tp)
                        k = act.activation(nat[j][:, HI, 2 * tp:2 * tp + 2, :],
                                           place(f"h{s}", j, tp)[:, :].rearrange("p (t d) -> p t d", t=2), ACT.Copy)
                        nat_hi[j].raised_by(k, f"h{s}{tp}")
                    for f in range(FT):
                        act.wait_ge(new_h[j].sem, new_h[j].at(f"h{s}{f}", it))
                        k = act.activation(feat[j][:, HI, f, :], h_v[j][:, f, :], ACT.Copy)
                        feat_hi[j].raised_by(k, f"h{s}{f}")

            with act.Fori(0, PASSES) as it:
                for unit in SCHEDULE:
                    kind, args = unit[0], unit[1:]
                    if kind == "scale":
                        scale(*args, it)
                    elif kind in ("ax", "x1T", "x3T"):
                        featured(*args, it, kind, kind[:2])
                    elif kind == "qkv":
                        qkv(*args, it)
                    elif kind == "attend":
                        attend(*args, it)
                    elif kind == "x2T":
                        x2T(*args, it)
                    elif kind == "adj_h":
                        s, j = args
                        evacuate_hi(j, it, (f"a{s}", j), lambda i: (qk_hi[j], f"a{s}{i}"), lambda i: ka[j][:, HI, i, :])
                    elif kind == "gates":
                        gates(*args, it)
                    elif kind == "update":
                        update(*args, it)
                    elif kind == "hT":
                        hT(*args, it)

        @block.vector
        def _(dve):
            def prep(instruction):
                instruction.then_inc(prep_dve, 1)

            dve.wait_ge(adj_loaded, 16)
            prep(dve.tensor_reduce(out=dinv[:, 0, :], in_=adj_n[:, :, :], axis=AX_X, op=ALU.add))
            dve.wait_ge(prep_dve, 1)
            prep(dve.tensor_scalar(dinv[:, 1, :], dinv[:, 0, :], 1e-37, None, ALU.max))
            prep(dve.tensor_scalar(dinv[:, 0, :], dinv[:, 0, :], 0.0, None, ALU.is_gt))
            prep(dve.tensor_scalar(mask1[:, :, :], adj_n[:, :, :], 0.0, MASKED, ALU.is_equal, ALU.mult))
            prep(dve.tensor_scalar(mask3[:, :, :], adj_n[:, :, :], 1.0, -FAR, ALU.subtract, ALU.mult))
            for m in range(NT):
                dve.wait_ge(prep_act, 1 + m)
                prep(dve.tensor_tensor(adjT[:, LO, m, :], bank[m][:, :], adjT[:, HI, m, :].bitcast(F32),
                                       ALU.subtract))
            dve.wait_ge(raw_loaded, RAW_LOADS)
            for name in ("q1", "q3"):
                c = col[name]
                prep(dve.tensor_scalar(raw[:, :, c:c + D], raw[:, :, c:c + D], -SCALE, None, ALU.mult))
            for i in range(3):
                prep(dve.tensor_tensor(raw_w[i][:, :, 0:D], raw_w[i][:, :, 0:D], raw_w[i][:, :, D:2 * D], ALU.add))
            prep(dve.tensor_scalar(raw_u[1], raw_u[1], 0.5, None, ALU.mult))
            prep(dve.tensor_scalar(cols[:, 0, :], cols[:, 0, :], -SCALE, None, ALU.mult))
            for a, b in ((2, 3), (4, 3), (5, 6)):
                prep(dve.tensor_tensor(cols[:, a, :], cols[:, a, :], cols[:, b, :], ALU.add))
            dve.wait_ge(prep_dve, 15 + NT)
            prep(dve.tensor_scalar(cols[:, 2:5:2, :], cols[:, 2:5:2, :], 0.5, None, ALU.mult))
            dve.wait_ge(prep_pool, 6)
            prep(dve.tensor_tensor(dinv[:, 0, :], dinv[:, 0, :], dinv[:, 2, :], ALU.mult))
            dve.wait_ge(prep_act, NT + 1)
            prep(dve.tensor_tensor(W[:, LO, :, 0:PLAIN], raw, W[:, HI, :, 0:PLAIN].bitcast(F32),
                                   ALU.subtract))
            for i, name in enumerate(("w3", "w4", "w5", "u3", "u5")):
                dve.wait_ge(prep_act, 2 + NT + i)
                c = col[name]
                prep(dve.tensor_tensor(W[:, LO, :, c:c + D],
                                       bank[(NT + i) % BANKS][:, :].rearrange("p (k c) -> p k c", k=FT),
                                       W[:, HI, :, c:c + D].bitcast(F32), ALU.subtract))

            aparts = [0]

            def apart():
                aparts[0] = (aparts[0] + 1) % SPARE
                dve.memset(spare[:, aparts[0]:aparts[0] + 1], 0.0)

            marks, o_added = [0], {}

            def mark(instruction):
                marks[0] += 1
                instruction.then_inc(dve_mark, 1)
                return marks[0]

            def wait_mark(m, it):
                dve.wait_ge(dve_mark, it * DVE_MARKS + m)

            def evacuate_lo(j, it, name, steps, dst, hi, bias=None):
                for i in range(2):
                    hi_sig, lo_sig, step = steps(i)
                    dve.wait_ge(hi_sig.sem, hi_sig.at(step, it))
                    src = place(*name, i)[:, :]
                    if bias is None:
                        k = dve.tensor_tensor(dst(i), src, hi(i).bitcast(F32), ALU.subtract)
                    else:
                        k = dve.scalar_tensor_tensor(dst(i), src, bias[:, i:i + 1], hi(i).bitcast(F32),
                                                     ALU.add, ALU.subtract)
                    lo_sig.raised_by(k, step)

            def featured(j, it, name, tag):
                evacuate_lo(j, it, (name, j), lambda i: (feat_hi[j], feat_lo[j], f"{tag}{i}"),
                            lambda i: feat[j][:, LO, i, :], lambda i: feat[j][:, HI, i, :])

            def moments(j, it, tag, tp, src, written):
                ms = []
                for t in (2 * tp, 2 * tp + 1):
                    step = f"{tag}{t}" if written is not o_ready[j] else f"o{tp}"
                    dve.wait_ge(written.sem, written.at(step, it))
                    ms.append(mark(dve.bn_stats(stats[j][:, t, :], src[:, t, :])))
                for t, m in zip((2 * tp, 2 * tp + 1), ms):
                    wait_mark(m, it)
                    apart()
                    k = dve.bn_aggr(mv[j][:, t, :], stats[j][:, t, :])
                var_ready[j].raised_by(k, f"{tag}{tp}")

            def normalize(j, it, tag):
                for tp in range(NT // 2):
                    dve.wait_ge(rstd_ready[j].sem, rstd_ready[j].at(f"{tag}{tp}", it))
                    for t in (2 * tp, 2 * tp + 1):
                        k = dve.tensor_scalar(res[j][:, t, :], res[j][:, t, :], mv[j][:, t, 0:1],
                                              rstd[j][:, t:t + 1], ALU.subtract, ALU.mult)
                        norm_ready[j].raised_by(k, f"{tag}{t}")

            def qkv(layer, j, it):
                for kind, buf, r in (("q", q_v[j], 0), ("k", ka[j], 1)):
                    evacuate_lo(j, it, (kind, layer, j), lambda i: (qk_hi[j], qk_lo[j], f"{kind}{layer}{i}"),
                                lambda i: buf[:, LO, i, :], lambda i: buf[:, HI, i, :],
                                bias=None if layer == 1 else cols[:, r, :])
                for tp in range(NT // 2):
                    wait_full(dve, it, "v", layer, j, tp)
                    src = place("v", layer, j, tp)[:, :].rearrange("p (t d) -> p t d", t=2)
                    dst = v_v[j][:, 2 * tp:2 * tp + 2, :]
                    if layer == 1:
                        k = dve.tensor_copy(dst, src)
                    else:
                        k = dve.tensor_tensor(dst, src, wide(4, 2), ALU.add)
                    v_ready[j].raised_by(k, f"v{layer}{tp}")

            def attend(layer, what, t, it):
                if what == "scores":
                    j, g, half, h, q = tile_of(t)
                    mask = mask1 if layer == 1 else mask3
                    wait_full(dve, it, "scores", layer, t)
                    if t >= P_RING:
                        wait_full(dve, it, "transpose", layer, t - P_RING)
                    apart()
                    k = dve.tensor_tensor_reduce(
                        out=probs[:, t % P_RING, :], in0=place("scores", layer, t)[:, :],
                        in1=mask[:, half * QT + q, :], scale=1.0, scalar=3.4e38, op0=ALU.add, op1=ALU.min,
                        accum_out=least[:, t % P_RING:t % P_RING + 1])
                    shifted.raised_by(k, f"{layer}.{t}")
                elif what == "transpose":
                    j, g, half, h, q = tile_of(t)
                    grp = t // GROUP
                    if t % 2:
                        wait_full(dve, it, "transpose", layer, t)
                        if grp >= 2:
                            wait_full(dve, it, "values", layer, grp - 2)
                        k = dve.tensor_copy(pt_v[:, grp % 2, h, :, q * P:(q + 1) * P],
                                            place("transpose", layer, t)[:, :].rearrange("p (k q) -> p k q", k=NT))
                        pt_dve.raised_by(k, f"{layer}.{t}")
                    if t % GROUP == GROUP - 1:
                        dve.wait_ge(exped.sem, exped.at(f"{layer}.{t}", it))
                        k = dve.reciprocal(recip[:, grp % 2, :], sums[:, grp % 2, :])
                        recip_ready.raised_by(k, f"{layer}.{grp}")
                else:
                    j, gh = divmod(t, GROUPS)
                    sl = slice(gh % HALVES * QH, (gh % HALVES + 1) * QH)
                    dve.wait_ge(rb_ready.sem, rb_ready.at(f"{layer}.{t}", it))
                    k = dve.tensor_tensor(o32[:, t % 2, :], place("values", layer, t)[:, 0:QH], o32[:, t % 2, :],
                                          ALU.mult)
                    o32_ready.raised_by(k, f"{layer}.{t}")
                    dve.wait_ge(feat_hi[j].sem, feat_hi[j].at(f"o{layer}{gh}", it))
                    k = dve.tensor_tensor(feat[j][:, LO, gh // HALVES, sl], o32[:, t % 2, :],
                                          feat[j][:, HI, gh // HALVES, sl].bitcast(F32), ALU.subtract)
                    feat_lo[j].raised_by(k, f"o{layer}{gh}")

            def residual(j, it, name, tag, after):
                dve.wait_ge(*after)
                for tp in range(NT // 2):
                    wait_full(dve, it, name, j, tp)
                    for i, t in enumerate((2 * tp, 2 * tp + 1)):
                        k = dve.tensor_tensor(res[j][:, t, :], place(name, j, tp)[:, i * D:(i + 1) * D],
                                              res[j][:, t, :], ALU.add)
                        summed[j].raised_by(k, f"{tag}{t}")
                    moments(j, it, tag, tp, res[j], summed[j])

            def scale(j, it):
                for t in range(NT):
                    dve.wait_ge(nat_hi[j].sem, nat_hi[j].at(f"x{t}", it))
                    k = dve.scalar_tensor_tensor(nat[j][:, LO, t, :], res[j][:, t, :], dinv[:, 0, t:t + 1],
                                                 nat[j][:, HI, t, :].bitcast(F32), ALU.mult, ALU.subtract)
                    nat_lo[j].raised_by(k, f"x{t}")

            def w0_norm(j, it):
                dve.wait_ge(biased[j].sem, biased[j].at("b0", it))
                for tp in range(NT // 2):
                    wait_full(dve, it, "w0", j, tp)
                    for i, t in enumerate((2 * tp, 2 * tp + 1)):
                        k = dve.scalar_tensor_tensor(res[j][:, t, :], place("w0", j, tp)[:, i * D:(i + 1) * D],
                                                     dinv[:, 0, t:t + 1], res[j][:, t, :], ALU.mult, ALU.add)
                        summed[j].raised_by(k, f"n0{t}")
                    moments(j, it, "n0", tp, res[j], summed[j])

            def proj1(j, it):
                for tp in range(NT // 2):
                    sl = slice(2 * tp, 2 * tp + 2)
                    wait_full(dve, it, "proj1", j, tp)
                    k = dve.tensor_tensor(v_v[j][:, sl, :],
                                          place("proj1", j, tp)[:, :].rearrange("p (t d) -> p t d", t=2),
                                          wide(1, 2), ALU.add)
                    o_ready[j].raised_by(k, f"o{tp}")
                for tp in range(NT // 2):
                    moments(j, it, "no", tp, v_v[j], o_ready[j])
                dve.wait_ge(biased[j].sem, biased[j].at("beta", it))
                for tp in range(NT // 2):
                    sl = slice(2 * tp, 2 * tp + 2)
                    o_added[j, tp] = mark(dve.tensor_tensor(res[j][:, sl, :], res[j][:, sl, :], v_v[j][:, sl, :],
                                                            ALU.add))

            def norm_o(j, it):
                for tp in range(NT // 2):
                    dve.wait_ge(rstd_ready[j].sem, rstd_ready[j].at(f"no{tp}", it))
                    wait_mark(o_added[j, tp], it)
                    ms = []
                    for t in (2 * tp, 2 * tp + 1):
                        ms.append(mark(dve.scalar_tensor_tensor(v_v[j][:, t, :], v_v[j][:, t, :], mv[j][:, t, 0:1],
                                                                rows[:, 2, :], ALU.subtract, ALU.mult)))
                    for t, m in zip((2 * tp, 2 * tp + 1), ms):
                        wait_mark(m, it)
                        k = dve.scalar_tensor_tensor(res[j][:, t, :], v_v[j][:, t, :], rstd[j][:, t:t + 1],
                                                     res[j][:, t, :], ALU.mult, ALU.add)
                        summed[j].raised_by(k, f"n1{t}")
                    moments(j, it, "n1", tp, res[j], summed[j])

            def x2T(j, it):
                dve.wait_ge(nat_hi[j].sem, nat_hi[j].at("rows2", it))
                k = dve.tensor_tensor(nat[j][:, LO, :, :], res[j][:, :, :], nat[j][:, HI, :, :].bitcast(F32),
                                      ALU.subtract)
                nat_lo[j].raised_by(k, "rows2")
                featured(j, it, "x2T", "x2")

            def gates(s, j, it):
                for f in range(FT):
                    dve.wait_ge(gate_r[j].sem, gate_r[j].at(f"r{s}{f}", it))
                    k = dve.scalar_tensor_tensor(tr(s, j)[:, f, :], tr(s, j)[:, f, :], 1.0, h_v[j][:, f, :],
                                                 ALU.add, ALU.mult)
                    reset[j].raised_by(k, f"r{s}{f}")

            def blend(s, f, j, it):
                dve.wait_ge(cand[j].sem, cand[j].at(f"c{s}{f}", it))
                m = mark(dve.tensor_tensor(tr(s, j)[:, f, :], tr(s, j)[:, f, :], h_v[j][:, f, :], ALU.subtract))
                wait_mark(m, it)
                m = mark(dve.scalar_tensor_tensor(tr(s, j)[:, f, :], tz(s, j)[:, f, :], 1.0, tr(s, j)[:, f, :],
                                                  ALU.add, ALU.mult))
                wait_mark(m, it)
                k = dve.scalar_tensor_tensor(h_v[j][:, f, :], tr(s, j)[:, f, :], 0.5, h_v[j][:, f, :],
                                             ALU.mult, ALU.add)
                new_h[j].raised_by(k, f"h{s}{f}")

            def hT(s, j, it):
                if s == GRU_STEPS - 1:
                    residual(j, it, f"h{s}", "n2", (norm_ready[j].sem, norm_ready[j].at(f"n1{NT - 1}", it)))
                    return
                for tp in range(NT // 2):
                    dve.wait_ge(nat_hi[j].sem, nat_hi[j].at(f"h{s}{tp}", it))
                    sl = slice(2 * tp, 2 * tp + 2)
                    k = dve.tensor_tensor(nat[j][:, LO, sl, :],
                                          place(f"h{s}", j, tp)[:, :].rearrange("p (t d) -> p t d", t=2),
                                          nat[j][:, HI, sl, :].bitcast(F32), ALU.subtract)
                    nat_lo[j].raised_by(k, f"h{s}{tp}")

            with dve.Fori(0, PASSES) as it:
                for unit in SCHEDULE:
                    kind, args = unit[0], unit[1:]
                    if kind == "scale":
                        scale(*args, it)
                    elif kind in ("ax", "x1T", "x3T"):
                        featured(*args, it, kind, kind[:2])
                    elif kind == "w0":
                        w0_norm(*args, it)
                    elif kind == "qkv":
                        qkv(*args, it)
                    elif kind == "attend":
                        attend(*args, it)
                    elif kind == "proj1":
                        proj1(*args, it)
                    elif kind == "norm_o":
                        norm_o(*args, it)
                    elif kind == "x2T":
                        x2T(*args, it)
                    elif kind == "adj_h":
                        s, j = args
                        evacuate_lo(j, it, (f"a{s}", j), lambda i: (qk_hi[j], qk_lo[j], f"a{s}{i}"),
                                    lambda i: ka[j][:, LO, i, :], lambda i: ka[j][:, HI, i, :])
                    elif kind == "gates":
                        gates(*args, it)
                    elif kind == "blend":
                        blend(*args, it)
                    elif kind == "hT":
                        hT(*args, it)
                    elif kind == "proj3":
                        j, = args
                        residual(j, it, "proj3", "n3", (biased[j].sem, biased[j].at("bo", it)))
                    elif kind in ("norm0", "norm1", "norm2", "norm3"):
                        normalize(*args, it, f"n{kind[-1]}")
            assert marks[0] == DVE_MARKS, marks[0]

        @block.tensor
        def _(pe):
            pe.wait_ge(prep_pool, 5)
            pe.wait_ge(adj_loaded, 16)
            for m in range(NT):
                for t in range(NT):
                    k = pe.transpose(bank[m][:, t * P:(t + 1) * P], adj_n[:, t, m * P:(m + 1) * P], ident[:, :])
                k.then_inc(prep_pe, 1)
            pe.wait_ge(prep_dve, 11 + NT)
            for i in range(5):
                w = raw_w[i] if i < 3 else raw_u[i - 3]
                b = NT + i
                for kt in range(FT):
                    for o in range(FT):
                        k = pe.transpose(bank[b % BANKS][:, kt * D + o * P:kt * D + (o + 1) * P],
                                         w[:, o, kt * P:(kt + 1) * P], ident[:, :])
                k.then_inc(prep_pe, 1)
            pe.wait_ge(prep_dve, PREP_DVE)

            def product(dst, a, b, start, stop):
                pe.matmul(dst, a(HI), b(LO), start=start, stop=False)
                pe.matmul(dst, a(HI), b(HI), start=False, stop=False)
                return pe.matmul(dst, a(LO), b(HI), start=False, stop=stop)

            def wait_sig(sig, step, it):
                pe.wait_ge(sig.sem, sig.at(step, it))

            def weight(name, kt, o=None):
                c = col[name]
                if o is None:
                    return lambda s: W[:, s, kt, c:c + D]
                return lambda s: W[:, s, kt, c + o * P:c + (o + 1) * P]

            def adj_product(j, it, name, steps):
                for f in range(FT):
                    wait_free(pe, it, name, j, f)
                    for m in range(NT):
                        if f == 0:
                            for step in steps[m]:
                                wait_sig(nat_lo[j], step, it)
                        k = product(place(name, j, f)[:, :], lambda s: nat[j][:, s, m, f * P:(f + 1) * P],
                                    lambda s: adjT[:, s, m, :], m == 0, m == NT - 1)
                    fill(k, name, j, f)

            def row_product(it, name, src, w, waits):
                for tp in range(NT // 2):
                    wait_free(pe, it, *name, tp)
                    for sig, step in waits(tp):
                        wait_sig(sig, step, it)
                    for i in range(2):
                        t = 2 * tp + i
                        for kt in range(FT):
                            k = product(place(*name, tp)[:, i * D:(i + 1) * D],
                                        lambda s: src[:, s, kt, t * P:(t + 1) * P], weight(w, kt),
                                        kt == 0, kt == FT - 1)
                    fill(k, *name, tp)

            def col_product(dst, src, w, o, start, stop):
                for kt in range(FT):
                    k = product(dst, weight(w, kt, o), lambda s: src[:, s, kt, :], start and kt == 0,
                                stop and kt == FT - 1)
                return k

            def rows_to_features(j, it, name, tag):
                for f in range(FT):
                    wait_free(pe, it, name, j, f)
                    for t in range(NT):
                        if f == 0:
                            wait_sig(norm_ready[j], f"{tag}{t}", it)
                        k = pe.transpose(place(name, j, f)[:, t * P:(t + 1) * P], res[j][:, t, f * P:(f + 1) * P],
                                         ident[:, :])
                    fill(k, name, j, f)

            def qkv(layer, j, it):
                wait_sig(feat_lo[j], f"x{layer}{FT - 1}", it)
                for kind in "qk":
                    for g in range(G):
                        wait_free(pe, it, kind, layer, j, g)
                        fill(col_product(place(kind, layer, j, g)[:, :], feat[j], f"{kind}{layer}", g, True, True),
                             kind, layer, j, g)
                row_product(it, ("v", layer, j), feat[j], f"v{layer}", lambda tp: ())

            def attend(layer, what, t, it):
                wait_free(pe, it, what, layer, t)
                dst = place(what, layer, t)
                if what == "scores":
                    j, g, half, h, q = tile_of(t)
                    if t % TILES == 0:
                        wait_sig(qk_lo[j], f"k{layer}{G - 1}", it)
                    rs = slice(HD * h, HD * (h + 1))
                    cs = slice((half * QT + q) * P, (half * QT + q + 1) * P)
                    k = product(dst[:, :], lambda s: q_v[j][rs, s, g, cs], lambda s: ka[j][rs, s, g, :],
                                True, True)
                elif what == "transpose":
                    wait_sig(exped, f"{layer}.{t}", it)
                    for m in range(NT):
                        k = pe.transpose(dst[:, m * P:(m + 1) * P], probs[:, t % P_RING, m * P:(m + 1) * P],
                                         ident[:, :])
                else:
                    j, gh = divmod(t, GROUPS)
                    g = gh // HALVES
                    last = (t + 1) * GROUP - 1
                    if gh == 0:
                        wait_sig(v_ready[j], f"v{layer}{NT // 2 - 1}", it)
                    wait_sig(rsum_ready, f"{layer}.{t}", it)
                    for q in range(QT):
                        pe.transpose(dst[:, QH + q * P:QH + (q + 1) * P], rsum[:, q, :], ident[:, :])
                    wait_sig(pt_act, f"{layer}.{last - 1}", it)
                    wait_sig(pt_dve, f"{layer}.{last}", it)
                    for m in range(NT):
                        for h in range(HG):
                            c = (g * HG + h) * HD
                            k = pe.matmul(dst[h * HD:(h + 1) * HD, 0:QH], v_v[j][:, m, c:c + HD],
                                          pt_v[:, t % 2, h, m, :], start=(m == 0), stop=(m == NT - 1))
                fill(k, what, layer, t)

            def gates(s, j, it):
                for kind in "zr":
                    for o in range(FT):
                        wait_free(pe, it, f"{kind}{s}", j, o)
                        if kind == "z" and o == 0:
                            if s == 0:
                                wait_sig(feat_lo[j], f"x2{FT - 1}", it)
                            else:
                                wait_sig(gru_lo[j], f"h{s - 1}{FT - 1}", it)
                        col_product(place(f"{kind}{s}", j, o)[:, :], feat[j], "u3", o, True, False)
                wait_sig(qk_lo[j], f"a{s}{FT - 1}", it)
                for kind, w in (("r", "w4"), ("z", "w3")):
                    for o in range(FT):
                        fill(col_product(place(f"{kind}{s}", j, o)[:, :], ka[j], w, o, False, True),
                             f"{kind}{s}", j, o)
                for o in range(FT):
                    wait_free(pe, it, f"c{s}", j, o)
                    col_product(place(f"c{s}", j, o)[:, :], ka[j], "w5", o, True, False)

            def update(s, j, it):
                wait_sig(gru_lo[j], f"r{s}{FT - 1}", it)
                for o in range(FT):
                    fill(col_product(place(f"c{s}", j, o)[:, :], feat[j], "u5", o, False, True), f"c{s}", j, o)

            def hT(s, j, it):
                for tp in range(NT // 2):
                    wait_free(pe, it, f"h{s}", j, tp)
                    for f in range(FT):
                        if tp == 0:
                            wait_sig(new_h[j], f"h{s}{f}", it)
                        for i in range(2):
                            t = 2 * tp + i
                            k = pe.transpose(place(f"h{s}", j, tp)[:, i * D + f * P:i * D + (f + 1) * P],
                                             h_v[j][:, f, t * P:(t + 1) * P], ident[:, :])
                    fill(k, f"h{s}", j, tp)

            with pe.Fori(0, PASSES) as it:
                for unit in SCHEDULE:
                    kind, args = unit[0], unit[1:]
                    if kind == "ax":
                        adj_product(*args, it, "ax", [[f"x{t}"] for t in range(NT)])
                    elif kind == "w0":
                        j, = args
                        row_product(it, ("w0", j), feat[j], "w0",
                                    lambda tp: [(feat_lo[j], f"ax{FT - 1}")] if tp == 0 else ())
                    elif kind in ("x1T", "x2T", "x3T"):
                        rows_to_features(*args, it, kind, {"x1T": "n0", "x2T": "n1", "x3T": "n2"}[kind])
                    elif kind == "qkv":
                        qkv(*args, it)
                    elif kind == "attend":
                        attend(*args, it)
                    elif kind in ("proj1", "proj3"):
                        j, = args
                        row_product(it, (kind, j), feat[j], f"o{kind[-1]}",
                                    lambda tp: [(feat_lo[j], f"o{kind[-1]}{GROUPS - 2 + tp}")])
                    elif kind == "adj_h":
                        s, j = args
                        adj_product(j, it, f"a{s}", [["rows2"]] + [[]] * (NT - 1) if s == 0 else
                                    [[f"h{s - 1}{t // 2}"] for t in range(NT)])
                    elif kind == "gates":
                        gates(*args, it)
                    elif kind == "update":
                        update(*args, it)
                    elif kind == "hT":
                        hT(*args, it)


_INS = ['x', 'adj', 'L0_gnn_weight', 'L0_gnn_bias', 'L1_gnn_w_qkv', 'L1_gnn_w_proj', 'L1_gnn_b_proj',
        'L1_gnn_ln_gamma', 'L1_gnn_ln_beta', 'L2_gnn_w3_w', 'L2_gnn_w3_b', 'L2_gnn_u3_w', 'L2_gnn_u3_b',
        'L2_gnn_w4_w', 'L2_gnn_w4_b', 'L2_gnn_w5_w', 'L2_gnn_w5_b', 'L2_gnn_u5_w', 'L2_gnn_u5_b', 'L3_gnn_Wq',
        'L3_gnn_bq', 'L3_gnn_Wk', 'L3_gnn_bk', 'L3_gnn_Wv', 'L3_gnn_bv', 'L3_gnn_Wo', 'L3_gnn_bo']


def kernel(**inputs):
    import numpy as _np
    import concourse.bacc as _bacc
    from concourse import mybir as _mybir
    from concourse.bass_utils import run_bass_kernel_spmd as _run

    nc = _bacc.Bacc("TRN2", target_bir_lowering=False, num_devices=1)
    arrays, args = {}, []
    for name in _INS:
        a = _np.ascontiguousarray(inputs[name])
        arrays[f"in_{name}_dram"] = a
        args.append(nc.dram_tensor(f"in_{name}_dram", a.shape, _mybir.dt.from_np(a.dtype), kind="ExternalInput").ap())
    shape = inputs["x"].shape
    args.append(nc.dram_tensor("out_dram", shape, _mybir.dt.float32, kind="ExternalOutput").ap())
    adj_resnorm_kernel(nc, *args)
    r = _run(nc, [arrays], core_ids=[0])
    return r.results[0]["out_dram"]
```
